# Optimizing a Trainium2 kernel written in Bass

```python
import numpy as np
import jax
import jax.numpy as jnp

def _softmax(x, axis=-1):
    return jax.nn.softmax(x, axis=axis)

def _gelu(x):
    return jax.nn.gelu(x, approximate=True)

def _silu(x):
    return jax.nn.silu(x)

def _sigmoid(x):
    return jax.nn.sigmoid(x)

def _layernorm(x, axis=-1, eps=1e-05):
    m = jnp.mean(x, axis=axis, keepdims=True)
    v = jnp.var(x, axis=axis, keepdims=True)
    return (x - m) / jnp.sqrt(v + eps)

def _scatter_add(tgt, idx, src, axis=0):
    return tgt.at[idx].add(src)

def _segment_sum(src, seg, n):
    return jax.ops.segment_sum(src, seg, n)
kernel_name = 'mk_gnn_preln_d2_gnn_r64_b1fb55'

def setup_inputs(seed: int=0):
    np.random.seed(seed)
    _w = jnp.asarray

    def _rec_inputs():
        import jax
        import jax.numpy as jnp
        _gk = jax.random.key(seed)
        x = -0.0002117 + 1 * jax.random.normal(jax.random.fold_in(_gk, 1), (10000, 512), jnp.float32)
        src = jax.random.randint(jax.random.fold_in(_gk, 2), (2500,), 0, 10000, jnp.int32)
        dst = jax.random.randint(jax.random.fold_in(_gk, 3), (2500,), 0, 10000, jnp.int32)
        _o = jnp.argsort(dst, stable=True)
        src = src[_o]
        dst = dst[_o]
        edge_type_3 = jax.random.randint(jax.random.fold_in(_gk, 12), (2500,), 0, 3, jnp.int32)
        return (x, src, dst, edge_type_3)
    x, src, dst, edge_type_3 = _rec_inputs()

    def _L0_gnn_setup():
        import jax, jax.numpy as jnp
        import numpy as np
        N_NODES = 50000
        N_EDGES = 156000
        D_IN = 512
        D_OUT = 512
        NUM_RELATIONS = 3
        EPS = 0.0
        key = jax.random.key(seed)
        ks = jax.random.split(key, 10)
        s = 1.0 / np.sqrt(D_IN)
        so = 1.0 / np.sqrt(D_OUT)
        return {'x': jax.random.normal(ks[0], (N_NODES, D_IN), dtype=jnp.float32), 'edge_index': jax.random.randint(ks[1], (2, N_EDGES), 0, N_NODES, dtype=jnp.int64), 'edge_type': jax.random.randint(ks[2], (N_EDGES,), 0, NUM_RELATIONS, dtype=jnp.int64), 'W_self': jax.random.uniform(ks[3], (D_IN, D_OUT), jnp.float32, -s, s), 'b_self': jax.random.uniform(ks[4], (D_OUT,), jnp.float32, -s, s), 'W1': jax.random.uniform(ks[5], (NUM_RELATIONS, D_IN, D_OUT), jnp.float32, -s, s), 'b1': jax.random.uniform(ks[6], (NUM_RELATIONS, D_OUT), jnp.float32, -s, s), 'W2': jax.random.uniform(ks[7], (NUM_RELATIONS, D_OUT, D_OUT), jnp.float32, -so, so), 'b2': jax.random.uniform(ks[8], (NUM_RELATIONS, D_OUT), jnp.float32, -so, so)}
    _L0_gnn_all = _L0_gnn_setup()
    _L0_gnn_in = {k: v for k, v in _L0_gnn_all.items() if k in ('W_self', 'b_self', 'W1', 'b1', 'W2', 'b2')}
    del _L0_gnn_all

    def _L1_gnn_setup():
        import jax, jax.numpy as jnp
        import numpy as np
        N_NODES = 100000
        N_EDGES = 12500
        DIM = 512
        key = jax.random.key(seed)
        k1, k2, k3, k4 = jax.random.split(key, 4)
        scale = 1.0 / np.sqrt(DIM)
        embedding = jax.random.normal(k1, (N_NODES, DIM), dtype=jnp.float32)
        edge_index = jax.random.randint(k2, (2, N_EDGES), 0, N_NODES, dtype=jnp.int64)
        W_gcn = jax.random.normal(k3, (DIM, DIM), dtype=jnp.float32) * scale
        b_gcn = jnp.zeros((DIM,), dtype=jnp.float32)
        W_dense = jax.random.normal(k4, (DIM, DIM), dtype=jnp.float32) * scale
        b_dense = jnp.zeros((DIM,), dtype=jnp.float32)
        return {'embedding': embedding, 'edge_index': edge_index, 'W_gcn': W_gcn, 'b_gcn': b_gcn, 'W_dense': W_dense, 'b_dense': b_dense}
    _L1_gnn_all = _L1_gnn_setup()
    _L1_gnn_in = {k: v for k, v in _L1_gnn_all.items() if k in ('W_gcn', 'b_gcn', 'W_dense', 'b_dense')}
    del _L1_gnn_all
    return {'x': x, 'src': src, 'dst': dst, 'edge_type_3': edge_type_3, 'L0_gnn_W_self': _L0_gnn_in['W_self'], 'L0_gnn_b_self': _L0_gnn_in['b_self'], 'L0_gnn_W1': _L0_gnn_in['W1'], 'L0_gnn_b1': _L0_gnn_in['b1'], 'L0_gnn_W2': _L0_gnn_in['W2'], 'L0_gnn_b2': _L0_gnn_in['b2'], 'L1_gnn_W_gcn': _L1_gnn_in['W_gcn'], 'L1_gnn_b_gcn': _L1_gnn_in['b_gcn'], 'L1_gnn_W_dense': _L1_gnn_in['W_dense'], 'L1_gnn_b_dense': _L1_gnn_in['b_dense']}

def reference(x, src, dst, edge_type_3, L0_gnn_W_self, L0_gnn_b_self, L0_gnn_W1, L0_gnn_b1, L0_gnn_W2, L0_gnn_b2, L1_gnn_W_gcn, L1_gnn_b_gcn, L1_gnn_W_dense, L1_gnn_b_dense):
    import jax
    import jax.numpy as jnp

    def _L0_gnn_ref(x, edge_index, edge_type, W_self, b_self, W1, b1, W2, b2):
        import jax, jax.numpy as jnp
        import numpy as np
        N_NODES = 50000
        N_EDGES = 156000
        D_IN = 512
        D_OUT = 512
        NUM_RELATIONS = 3
        EPS = 0.0
        n_nodes = x.shape[0]
        src, dst = (edge_index[0], edge_index[1])
        x_src = x[src]
        out = x @ W_self + b_self
        for r in range(NUM_RELATIONS):
            mask = (edge_type == r).astype(x.dtype)[:, None]
            agg = jax.ops.segment_sum(x_src * mask, dst, num_segments=n_nodes)
            h = (1.0 + EPS) * x + agg
            h = jnp.maximum(h @ W1[r] + b1[r], 0.0) @ W2[r] + b2[r]
            out = out + h
        return out

    def _L1_gnn_ref(embedding, edge_index, W_gcn, b_gcn, W_dense, b_dense):
        import jax, jax.numpy as jnp
        import numpy as np
        N_NODES = 100000
        N_EDGES = 12500
        DIM = 512
        N = embedding.shape[0]
        loop = jnp.arange(N, dtype=edge_index.dtype)
        src = jnp.concatenate([edge_index[0], loop])
        dst = jnp.concatenate([edge_index[1], loop])
        deg = jax.ops.segment_sum(jnp.ones_like(dst, dtype=embedding.dtype), dst, num_segments=N)
        dinv = jnp.where(deg > 0, jax.lax.rsqrt(deg), 0.0)
        norm = dinv[src] * dinv[dst]
        h = embedding @ W_gcn
        msg = h[src] * norm[:, None]
        agg = jax.ops.segment_sum(msg, dst, num_segments=N) + b_gcn
        return agg @ W_dense + b_dense
    edge_index = jnp.stack([src, dst])
    h = jnp.maximum(_layernorm(x, axis=-1), 0.0)
    x = x + _L0_gnn_ref(h, edge_index, edge_type_3, L0_gnn_W_self, L0_gnn_b_self, L0_gnn_W1, L0_gnn_b1, L0_gnn_W2, L0_gnn_b2)
    h = jnp.maximum(_layernorm(x, axis=-1), 0.0)
    x = x + _L1_gnn_ref(h, edge_index, L1_gnn_W_gcn, L1_gnn_b_gcn, L1_gnn_W_dense, L1_gnn_b_dense)
    return x

_drawn_inputs = setup_inputs


def setup_inputs(seed=0):
    import zlib

    import numpy as np

    out = dict(_drawn_inputs(seed))
    spreads = {'L1_gnn_b_gcn': (0.0, 0.1), 'L1_gnn_b_dense': (0.0, 0.1)}
    factors = {'L0_gnn_b1': 3.463}
    for name, (base, spread) in spreads.items():
        noise = np.random.default_rng([zlib.crc32(name.encode()), seed]).standard_normal(out[name].shape)
        drawn = base * np.exp(spread * noise) if base else spread * noise
        out[name] = jnp.asarray(drawn.astype(out[name].dtype))
    for name, factor in factors.items():
        out[name] = (out[name] * factor).astype(out[name].dtype)
    return out
```

```python
from contextlib import ExitStack

import concourse.bass as bass
from concourse import mybir


def build_program(nc, x, src, dst, edge_type, w_self, b_self, w1, b1, w2, b2, w_gcn, b_gcn, w_dense, b_dense, out):
    F32, F32R, BF16, I32 = mybir.dt.float32, mybir.dt.float32r, mybir.dt.bfloat16, mybir.dt.int32
    ALU, ACT, AX = mybir.AluOpType, mybir.ActivationFunctionType, mybir.AxisListType

    N, D = x.shape
    E = src.shape[0]
    R = w1.shape[0]
    P, J = 125, 4
    BN = P * J
    NB = N // BN
    KC = D // 128
    W = NB * R
    EJ = E // P
    SLOTS = 64
    MAXR = -(-E // SLOTS)
    XW = D + 4
    EPS = 1e-5
    ROUND = 12582912.0
    ABSENT = 20000.0
    STEPS = R * KC
    assert NB * BN == N and KC * 128 == D and EJ * P == E
    PARTS = ((0, 112), (112, P))

    x_blocks = x.rearrange("(b p j) d -> b p j d", p=P, j=J)
    out_blocks = out.rearrange("(b p j) d -> b p j d", p=P, j=J)
    mid = nc.dram_tensor("mid", [N, XW], F32, kind="Internal").ap()
    mid_blocks = mid.rearrange("(b p j) d -> b p j d", p=P, j=J)
    fused_dram = nc.dram_tensor("fused_w", [128, KC * D], F32, kind="Internal").ap()
    bias2_dram = nc.dram_tensor("bias2", [128, D], F32, kind="Internal").ap()
    slot_src_dram = nc.dram_tensor("slot_src", [MAXR, 128, W], I32, kind="Internal").ap()
    slot_col_dram = nc.dram_tensor("slot_col", [MAXR, 128, W], F32, kind="Internal").ap()

    class Chain:

        def __init__(self, engine, sem, at=0):
            self.engine, self.sem, self.at, self.n = engine, sem, at, 0

        def link(self, instruction):
            self.n += 1
            instruction.then_inc(self.sem, 1)
            self.engine.wait_ge(self.sem, self.at + self.n)

    with ExitStack() as ctx:
        def sb(name, shape, dt=F32, into=ctx):
            return into.enter_context(nc.sbuf_tensor(name, shape, dt))

        def sem(name):
            return ctx.enter_context(nc.semaphore(name))

        ws_hi, ws_lo = sb("ws_hi", [128, KC, D], F32R), sb("ws_lo", [128, KC, D], F32R)
        bias = sb("bias", [128, D])
        b1_col = sb("b1_col", [128, STEPS])
        ident = sb("ident", [128, 128])
        node_iota = sb("node_iota", [128, BN])
        dinv = sb("dinv", [P, NB * J])
        slot_src = sb("slot_src_sb", [128, W], I32)
        slot_col = sb("slot_col_sb", [128, W])
        rounds_sb = sb("rounds_sb", [128, 1], I32)

        layer0 = ExitStack()
        w1_hi, w1_lo = sb("w1_hi", [128, R * KC, D], F32R, layer0), sb("w1_lo", [128, R * KC, D], F32R, layer0)
        w2_hi, w2_lo = sb("w2_hi", [128, R * KC, D], F32R, layer0), sb("w2_lo", [128, R * KC, D], F32R, layer0)

        prep = ExitStack()
        with prep:
            def tmp(name, shape, dt=F32):
                return sb(name, shape, dt, prep)

            stage = [tmp(f"stage{i}", [128, KC, D]) for i in range(2)]
            gcn, gcn_t, dense = tmp("gcn", [128, KC, D]), tmp("gcn_t", [128, KC, D]), tmp("dense", [128, KC, D])
            ints = tmp("ints", [P, 3, EJ], I32)
            srcf, dstf, typef = (tmp(n, [P, EJ]) for n in ("srcf", "dstf", "typef"))
            blk, loc, prt, row4, col, bucket, qidx, rank = (
                tmp(n, [P, EJ]) for n in ("blk", "loc", "prt", "row4", "col", "bucket", "qidx", "rank"))
            hot = tmp("hot", [P, EJ, W])
            before = tmp("before", [P, EJ, W])
            pairs = tmp("pairs", [P, EJ, 2, W])
            pick = tmp("pick", [P, EJ, 128])
            hot_p, hot_q = tmp("hot_p", [P, EJ, P], BF16), tmp("hot_q", [P, EJ, NB * J], BF16)
            row_sum = tmp("row_sum", [P, W])
            iota_w, iota_p, iota_q, iota_s = (
                tmp(n, [P, k]) for n, k in (("iota_w", W), ("iota_p", P), ("iota_q", NB * J), ("iota_s", 128)))
            tri = tmp("tri", [P, P])
            ones = tmp("ones", [P, 128])
            b1_rows, bg_rows = tmp("b1_rows", [STEPS, 128]), tmp("bg_rows", [KC, 128])
            bg_col = tmp("bg_col", [128, KC])
            bias_rows, dense_row = tmp("bias_rows", [R + 1, D]), tmp("dense_row", [1, D])
            bias2 = tmp("bias2_sb", [128, D])
            deg, root, y2 = tmp("deg", [P, NB * J]), tmp("root", [P, NB * J]), tmp("y2", [P, NB * J])
            top = tmp("top", [128, 2])
            empty = tmp("empty", [128, W])
            psum = ExitStack()
            with psum:
                def pb(name, shape):
                    return psum.enter_context(nc.psum_tensor(name, shape, F32))

                p_rank, p_count, p_slots, p_deg, p_cols = (
                    pb(n, [128, 512]) for n in ("p_rank", "p_count", "p_slots", "p_deg", "p_cols"))
                p_fuse = [pb(f"p_fuse{i}", [128, 512]) for i in range(3)]

                edges_in, consts, w_in = sem("edges_in"), sem("consts"), [sem("w_in0"), sem("w_in1")]
                fuse_in, bias_in = sem("fuse_in"), sem("bias_in")
                chain_p, chain_g = sem("chain_p"), sem("chain_g")
                w_high, w_split = sem("w_high"), sem("w_split")
                sums_ready, ranks_up, picked, slots_up = (
                    sem("sums_ready"), sem("ranks_up"), sem("picked"), sem("slots_up"))
                slots_out, slots_stored, slots_back = sem("slots_out"), sem("slots_stored"), sem("slots_back")
                hots_ready, deg_up, deg_ready, root_ready = (
                    sem("hots_ready"), sem("deg_up"), sem("deg_ready"), sem("root_ready"))
                rounds_ready = sem("rounds_ready")
                cols_up, cols_copied = sem("cols_up"), sem("cols_copied")
                gt_up, gt_copied, fused_up, fused_copied, fused_out = (
                    sem("gt_up"), sem("gt_copied"), sem("fused_up"), sem("fused_copied"), sem("fused_out"))
                bias_up, bias2_up, bias2_copied = sem("bias_up"), sem("bias2_up"), sem("bias2_copied")

                weights = ([(w_self, ws_hi, ws_lo, 0)] + [(w1[r], w1_hi, w1_lo, r * KC) for r in range(R)]
                           + [(w2[r], w2_hi, w2_lo, r * KC) for r in range(R)])

                with nc.Block() as block:
                    @block.sync
                    def _(sp):
                        for i, a in enumerate((dst, edge_type, src)):
                            sp.dma_start(ints[:, i, :], a.rearrange("(p i) -> p i", p=P)).then_inc(edges_in, 16)
                        for i, (w, _, _, _) in enumerate(weights):
                            if i >= 2:
                                sp.wait_ge(w_split, i - 1)
                            sp.dma_start(stage[i % 2][:, :, :], w.rearrange("(k p) n -> p k n", p=128))\
                                .then_inc(w_in[i % 2], 16)
                        sp.wait_ge(rounds_ready, 1)
                        rounds = sp.value_load(rounds_sb[0:1, 0:1], min_val=0, max_val=MAXR - 1)
                        sp.wait_ge(slots_stored, 32 * (rounds + 1))
                        sp.dma_start(slot_src[:, :], slot_src_dram[0]).then_inc(slots_back, 16)
                        sp.dma_start(slot_col[:, :], slot_col_dram[0]).then_inc(slots_back, 16)
                        sp.wait_ge(slots_back, 32)
                        sp.wait_ge(fused_copied, KC)
                        sp.dma_start(fused_dram, gcn[:, :, :].rearrange("p k n -> p (k n)")).then_inc(fused_out, 16)
                        sp.wait_ge(bias2_copied, 1)
                        sp.dma_start(bias2_dram, bias2[:, :]).then_inc(fused_out, 16)
                        sp.wait_ge(fused_out, 32)

                    @block.gpsimd
                    def _(pool):
                        link = Chain(pool, chain_g).link
                        for t, k in ((iota_w, W), (iota_p, P), (iota_q, NB * J)):
                            pool.iota(t[:, :], [[1, k]], base=0, channel_multiplier=0,
                                      allow_small_or_imprecise_dtypes=True)
                        pool.iota(iota_s[:, :].rearrange("p (a s) -> p a s", a=2), [[0, 2], [1, SLOTS]], base=0,
                                  channel_multiplier=0, allow_small_or_imprecise_dtypes=True)
                        pool.iota(node_iota[:, :], [[1, BN]], base=0, channel_multiplier=0,
                                  allow_small_or_imprecise_dtypes=True)
                        pool.memset(ones[:, :], 1.0)
                        pool.memset(tri[:, :], 1.0)
                        link(pool.memset(ident[:, :], 0.0))
                        link(pool.affine_select(out=ident[:, :], in_=ident[:, :], compare_op=ALU.not_equal, fill=1.0,
                                                base=0, pattern=[[-1, 128]], channel_multiplier=1))
                        pool.affine_select(out=tri[:, :], in_=tri[:, :], compare_op=ALU.is_ge, fill=0.0,
                                           base=-1, pattern=[[1, P]], channel_multiplier=-1).then_inc(consts, 1)
                        pool.wait_ge(rounds_ready, 1)
                        rounds = pool.value_load(rounds_sb[0:1, 0:1], min_val=0, max_val=MAXR - 1)
                        with pool.Fori(0, rounds + 1) as k:
                            pool.wait_ge(slots_out, 4 * (k + 1))
                            pool.dma_start(slot_src_dram[k], slot_src[:, :]).then_inc(slots_stored, 16)
                            pool.dma_start(slot_col_dram[k], slot_col[:, :]).then_inc(slots_stored, 16)

                    @block.scalar
                    def _(act):
                        act.dma_start(gcn[:, :, :], w_gcn.rearrange("(k p) n -> p k n", p=128)).then_inc(fuse_in, 16)
                        act.dma_start(dense[:, :, :], w_dense.rearrange("(k p) n -> p k n", p=128))\
                            .then_inc(fuse_in, 16)
                        act.dma_start(b1_rows[:, :], b1.rearrange("r (m p) -> (r m) p", p=128)).then_inc(bias_in, 16)
                        act.dma_start(bg_rows[:, :], b_gcn.rearrange("(m p) -> m p", p=128)).then_inc(bias_in, 16)
                        act.dma_start(bias_rows[0:1, :], b_self[None, :]).then_inc(bias_in, 16)
                        act.dma_start(bias_rows[1:R + 1, :], b2).then_inc(bias_in, 16)
                        act.dma_start(dense_row[:, :], b_dense[None, :]).then_inc(bias_in, 16)

                        def high(i):
                            _, hi, _, at = weights[i]
                            act.wait_ge(w_in[i % 2], 16 * (i // 2 + 1))
                            act.activation(hi[:, at:at + KC, :], stage[i % 2][:, :, :], ACT.Copy).then_inc(w_high, 1)

                        high(0)
                        act.wait_ge(deg_ready, 1)
                        act.activation(root[:, :], deg[:, :], ACT.Sqrt).then_inc(root_ready, 1)
                        high(1)
                        for k in range(KC):
                            act.wait_ge(gt_up, k + 1)
                            act.activation(gcn_t[:, k, :], p_fuse[k % 2][:, :], ACT.Copy).then_inc(gt_copied, 1)
                        high(2)
                        for m in range(KC):
                            act.wait_ge(fused_up, m + 1)
                            act.activation(gcn[:, m, :], p_fuse[m % 2][:, :], ACT.Copy).then_inc(fused_copied, 1)
                        for i in range(3, len(weights)):
                            high(i)

                    @block.vector
                    def _(dve):
                        link = Chain(dve, chain_p).link

                        def low(i):
                            _, hi, lo, at = weights[i]
                            dve.wait_ge(w_high, i + 1)
                            dve.tensor_tensor(lo[:, at:at + KC, :], stage[i % 2][:, :, :],
                                              hi[:, at:at + KC, :].bitcast(F32), ALU.subtract).then_inc(w_split, 1)

                        def floor_div(to, scratch, a, by, mid_point):
                            link(dve.tensor_scalar(scratch[:, :], a[:, :], mid_point, 1.0 / by, ALU.subtract, ALU.mult))
                            link(dve.tensor_scalar(to[:, :], scratch[:, :], ROUND, ROUND, ALU.add, ALU.subtract))

                        def fma(to, a, by, plus):
                            link(dve.scalar_tensor_tensor(to[:, :], a[:, :], by, plus[:, :], ALU.mult, ALU.add))

                        dve.wait_ge(edges_in, 48)
                        dve.tensor_copy(dstf[:, :], ints[:, 0, :])
                        dve.tensor_copy(typef[:, :], ints[:, 1, :])
                        link(dve.tensor_copy(srcf[:, :], ints[:, 2, :]))
                        floor_div(blk, rank, dstf, BN, (BN - 1) / 2)
                        fma(loc, blk, -float(BN), dstf)
                        floor_div(prt, rank, loc, J, (J - 1) / 2)
                        fma(row4, prt, -float(J), loc)
                        fma(col, row4, float(P), prt)
                        fma(bucket, blk, float(R), typef)
                        fma(qidx, blk, float(J), row4)
                        dve.wait_ge(consts, 1)

                        def one_hot(to, iota, k, a):
                            return dve.tensor_tensor(
                                to[:, :, :], iota[:, :].unsqueeze(1).to_broadcast([P, EJ, k]),
                                a[:, :].unsqueeze(2).to_broadcast([P, EJ, k]), ALU.is_equal)

                        link(one_hot(hot, iota_w, W, bucket))
                        link(dve.memset(before[:, 0, :], 0.0))
                        for i in range(1, EJ):
                            link(dve.tensor_tensor(before[:, i, :], before[:, i - 1, :], hot[:, i - 1, :], ALU.add))
                        dve.tensor_tensor(row_sum[:, :], before[:, EJ - 1, :], hot[:, EJ - 1, :], ALU.add)\
                            .then_inc(sums_ready, 1)
                        one_hot(hot_p, iota_p, P, prt)
                        one_hot(hot_q, iota_q, NB * J, qidx).then_inc(hots_ready, 1)
                        link(dve.scalar_tensor_tensor(
                            pairs[:, :, 0, :], srcf[:, :].unsqueeze(2).to_broadcast([P, EJ, W]), 1.0,
                            hot[:, :, :], ALU.add, ALU.mult))
                        link(dve.scalar_tensor_tensor(
                            pairs[:, :, 1, :], col[:, :].unsqueeze(2).to_broadcast([P, EJ, W]), 1.0,
                            hot[:, :, :], ALU.add, ALU.mult))
                        dve.wait_ge(ranks_up, 1)
                        link(dve.tensor_tensor(before[:, :, :], before[:, :, :],
                                               p_rank[0:P, 0:W].unsqueeze(1).to_broadcast([P, EJ, W]), ALU.add))
                        link(dve.tensor_tensor(before[:, :, :], before[:, :, :], hot[:, :, :], ALU.mult))
                        link(dve.tensor_reduce(rank[:, :], before[:, :, :], AX.X, ALU.add))
                        dve.wait_ge(ranks_up, 2)
                        link(dve.tensor_reduce(top[:, 0:1], p_count[:, 0:W], AX.X, ALU.max))
                        link(dve.tensor_scalar(top[:, 1:2], top[:, 0:1], (SLOTS - 1) / 2, 1.0 / SLOTS,
                                               ALU.add, ALU.mult))
                        link(dve.tensor_scalar(top[:, 0:1], top[:, 1:2], ROUND, ROUND, ALU.add, ALU.subtract))
                        dve.tensor_scalar(rounds_sb[:, :], top[:, 0:1], -1.0, 0.0, ALU.add, ALU.max).then_inc(rounds_ready, 1)
                        dve.wait_ge(deg_up, 1)
                        dve.tensor_scalar(deg[:, :], p_deg[0:P, 0:NB * J], 1.0, None, ALU.add).then_inc(deg_ready, 1)
                        dve.wait_ge(root_ready, 1)
                        link(dve.reciprocal(dinv[:, :], root[:, :]))
                        link(dve.tensor_tensor(y2[:, :], dinv[:, :], dinv[:, :], ALU.mult))
                        link(dve.tensor_tensor(y2[:, :], y2[:, :], deg[:, :], ALU.mult))
                        link(dve.tensor_scalar(y2[:, :], y2[:, :], -0.5, 1.5, ALU.mult, ALU.add))
                        link(dve.tensor_tensor(dinv[:, :], dinv[:, :], y2[:, :], ALU.mult))
                        dve.wait_ge(rounds_ready, 1)
                        rounds = dve.value_load(rounds_sb[0:1, 0:1], min_val=0, max_val=MAXR - 1)
                        with dve.Fori(0, rounds + 1) as k:
                            dve.tensor_tensor(pick[:, :, :], iota_s[:, :].unsqueeze(1).to_broadcast([P, EJ, 128]),
                                              rank[:, :].unsqueeze(2).to_broadcast([P, EJ, 128]), ALU.is_equal)\
                                .then_inc(picked, 1)
                            dve.wait_ge(slots_up, k + 1)
                            dve.wait_ge(slots_stored, 32 * k)
                            inner = Chain(dve, slots_out, 4 * k).link
                            inner(dve.tensor_scalar(empty[:, :], p_slots[:, 0:W], 0.0, ABSENT, ALU.is_equal, ALU.mult))
                            inner(dve.scalar_tensor_tensor(slot_src[:, :], p_slots[:, 0:W], -1.0, empty[:, :],
                                                           ALU.add, ALU.add))
                            inner(dve.tensor_scalar(slot_col[:, :], p_slots[:, W:2 * W], -1.0, None, ALU.add))
                            inner(dve.tensor_scalar(rank[:, :], rank[:, :], -float(SLOTS), None, ALU.add))
                        low(0)
                        dve.wait_ge(cols_up, 1)
                        dve.tensor_copy(b1_col[:, :], p_cols[:, 0:STEPS])
                        dve.tensor_copy(bg_col[:, :], p_cols[:, 16:16 + KC]).then_inc(cols_copied, 1)
                        low(1)
                        dve.wait_ge(bias_up, 1)
                        dve.tensor_copy(bias[:, :], p_count[:, :])
                        low(2)
                        dve.wait_ge(bias2_up, 1)
                        dve.tensor_copy(bias2[:, :], p_fuse[2][:, :]).then_inc(bias2_copied, 1)
                        for i in range(3, len(weights)):
                            low(i)

                    @block.tensor
                    def _(pe):
                        pe.wait_ge(consts, 1)
                        pe.wait_ge(sums_ready, 1)
                        pe.matmul(p_rank[0:P, 0:W], tri[:, :], row_sum[:, :], start=True, stop=True)\
                            .then_inc(ranks_up, 1)
                        pe.matmul(p_count[:, 0:W], ones[:, :], row_sum[:, :], start=True, stop=True)\
                            .then_inc(ranks_up, 1)
                        pe.wait_ge(hots_ready, 1)
                        for i in range(EJ):
                            mm = pe.matmul(p_deg[0:P, 0:NB * J], hot_p[:, i, :], hot_q[:, i, :],
                                           start=(i == 0), stop=(i == EJ - 1))
                        mm.then_inc(deg_up, 1)
                        pe.wait_ge(rounds_ready, 1)
                        rounds = pe.value_load(rounds_sb[0:1, 0:1], min_val=0, max_val=MAXR - 1)
                        with pe.Fori(0, rounds + 1) as k:
                            pe.wait_ge(picked, k + 1)
                            for i in range(EJ):
                                mm = pe.matmul(p_slots[:, 0:2 * W], pick[:, i, :],
                                               pairs[:, i, :, :].rearrange("p a w -> p (a w)"),
                                               start=(i == 0), stop=(i == EJ - 1))
                            mm.then_inc(slots_up, 1)
                        pe.wait_ge(bias_in, 16 * 5)
                        pe.transpose(p_cols[:, 0:STEPS], b1_rows[:, :], ident[0:STEPS, 0:STEPS])
                        pe.transpose(p_cols[:, 16:16 + KC], bg_rows[:, :], ident[0:KC, 0:KC]).then_inc(cols_up, 1)
                        pe.matmul(p_count[:, :], ones[0:R + 1, :], bias_rows[:, :], start=True, stop=True)\
                            .then_inc(bias_up, 1)
                        pe.wait_ge(fuse_in, 32)
                        for k in range(KC):
                            if k >= 2:
                                pe.wait_ge(gt_copied, k - 1)
                            for m in range(KC):
                                mm = pe.transpose(p_fuse[k % 2][:, m * 128:(m + 1) * 128],
                                                  gcn[:, m, k * 128:(k + 1) * 128], ident[:, :])
                            mm.then_inc(gt_up, 1)
                        for m in range(KC):
                            pe.wait_ge(gt_copied, KC)
                            if m >= 2:
                                pe.wait_ge(fused_copied, m - 1)
                            for k in range(KC):
                                mm = pe.matmul(p_fuse[m % 2][:, :], gcn_t[:, k, m * 128:(m + 1) * 128], dense[:, k, :],
                                               start=(k == 0), stop=(k == KC - 1))
                            mm.then_inc(fused_up, 1)
                        pe.wait_ge(cols_copied, 1)
                        for k in range(KC):
                            pe.matmul(p_fuse[2][:, :], bg_col[:, k:k + 1].to_broadcast([128, 128]),
                                      dense[:, k, :], start=(k == 0), stop=False)
                        pe.matmul(p_fuse[2][:, :], ones[0:1, :], dense_row[:, :], start=False, stop=True)\
                            .then_inc(bias2_up, 1)

        class Rows:
            LINKS = 7

            def __init__(self, name, into, degree, share=None):
                self.degree = degree
                if share:
                    self.x, self.xr, self.select, self.small = share.x, share.xr, share.select, share.small
                else:
                    self.x = sb(name + "_x", [128, XW], F32, into)
                    self.xr = sb(name + "_xr", [128, D], F32R, into)
                    self.select = sb(name + "_select", [128, BN], F32R, into)
                    self.small = sb(name + "_small", [128, 16], F32, into)
                self.gathered, self.chain = sem(name + "_gathered"), sem(name + "_chain")
                self.var_ready, self.root_ready = sem(name + "_var_ready"), sem(name + "_root_ready")
                self.norm_ready, self.relued = sem(name + "_norm_ready"), sem(name + "_relued")
                self.high_ready, self.ready = sem(name + "_high_ready"), sem(name + "_ready")

            def on_vector(self, dve, n, column):
                link = Chain(dve, self.chain, (self.LINKS + self.degree) * n).link
                stat, mean, var = self.small[:, 0:6], self.small[:, 6:7], self.small[:, 7:8]
                v, root, y, t, shift = (self.small[:, i:i + 1] for i in range(8, 13))
                dve.wait_ge(self.gathered, 16 * (n + 1))
                link(dve.bn_stats(stat, self.x[:, 0:D]))
                dve.tensor_scalar(self.select[:, :], node_iota[:, :], column, None, ALU.is_equal)
                link(dve.bn_aggr(self.small[:, 6:8], stat))
                dve.tensor_scalar(v, var, EPS, None, ALU.add).then_inc(self.var_ready, 1)
                dve.wait_ge(self.root_ready, n + 1)
                link(dve.reciprocal(y, root))
                link(dve.tensor_tensor(t, y, y, ALU.mult))
                link(dve.tensor_tensor(t, t, v, ALU.mult))
                link(dve.tensor_scalar(t, t, -0.5, 1.5, ALU.mult, ALU.add))
                link(dve.tensor_tensor(y, y, t, ALU.mult))
                if self.degree:
                    link(dve.tensor_tensor(y, y, self.x[:, D:D + 1], ALU.mult))
                dve.scalar_tensor_tensor(shift, mean, -1.0, y, ALU.mult, ALU.mult).then_inc(self.norm_ready, 1)
                dve.wait_ge(self.high_ready, n + 1)
                dve.tensor_tensor(self.xr[SLOTS:128, :], self.x[SLOTS:128, 0:D], self.xr[SLOTS:128, :].bitcast(F32),
                                  ALU.subtract).then_inc(self.ready, 1)

            def on_scalar(self, act, n):
                v, root, y, t, shift = (self.small[:, i:i + 1] for i in range(8, 13))
                act.wait_ge(self.var_ready, n + 1)
                act.activation(root, v, ACT.Sqrt).then_inc(self.root_ready, 1)
                act.wait_ge(self.norm_ready, n + 1)
                act.activation(self.x[:, 0:D], self.x[:, 0:D], ACT.Relu, bias=shift, scale=y).then_inc(self.relued, 1)
                act.wait_ge(self.relued, n + 1)
                act.activation(self.xr[:, :], self.x[:, 0:D], ACT.Copy).then_inc(self.high_ready, 1)

        class Nodes:
            LINKS = 7

            def __init__(self, name, into, degree):
                self.degree = degree
                self.stat = sb(name + "_stat", [P, J, 6], F32, into)
                self.mean_var = sb(name + "_mean_var", [P, J, 2], F32, into)
                self.v, self.root, self.y, self.t, self.shift = (
                    sb(name + n, [P, J], F32, into) for n in ("_v", "_root", "_y", "_t", "_shift"))
                self.chain, self.var_ready, self.root_ready = (
                    sem(name + "_chain"), sem(name + "_var_ready"), sem(name + "_root_ready"))
                self.norm_ready, self.ready = sem(name + "_norm_ready"), sem(name + "_ready")

            def on_vector(self, dve, b, source):
                link = Chain(dve, self.chain, (self.LINKS + self.degree) * b).link
                for j in range(J):
                    step = dve.bn_stats(self.stat[:, j, :], source[:, j, 0:D])
                link(step)
                dve.memset(self.t[:, :], 0.0)
                for j in range(J):
                    step = dve.bn_aggr(self.mean_var[:, j, :], self.stat[:, j, :])
                link(step)
                dve.tensor_scalar(self.v[:, :], self.mean_var[:, :, 1], EPS, None, ALU.add)\
                    .then_inc(self.var_ready, 1)
                dve.wait_ge(self.root_ready, b + 1)
                y, t = self.y[:, :], self.t[:, :]
                link(dve.reciprocal(y, self.root[:, :]))
                link(dve.tensor_tensor(t, y, y, ALU.mult))
                link(dve.tensor_tensor(t, t, self.v[:, :], ALU.mult))
                link(dve.tensor_scalar(t, t, -0.5, 1.5, ALU.mult, ALU.add))
                link(dve.tensor_tensor(y, y, t, ALU.mult))
                if self.degree:
                    link(dve.tensor_tensor(y, y, source[:, :, D], ALU.mult))
                dve.scalar_tensor_tensor(self.shift[:, :], self.mean_var[:, :, 0], -1.0, y, ALU.mult, ALU.mult)\
                    .then_inc(self.norm_ready, 1)

            def on_scalar(self, act, b, source, h):
                act.wait_ge(self.var_ready, b + 1)
                act.activation(self.root[:, :], self.v[:, :], ACT.Sqrt).then_inc(self.root_ready, 1)
                act.wait_ge(self.norm_ready, b + 1)
                for j in range(J):
                    act.activation(h[:, j, :], source[:, j, 0:D], ACT.Relu, bias=self.shift[:, j:j + 1],
                                   scale=self.y[:, j:j + 1]).then_inc(self.ready, 1)

        def split_product(pe, bank, stationary, moving, start, stop):
            (s_hi, s_lo), (m_hi, m_lo) = stationary, moving
            pe.matmul(bank, s_hi, m_hi, start=start, stop=False)
            pe.matmul(bank, s_hi, m_lo, start=False, stop=False)
            return pe.matmul(bank, s_lo, m_hi, start=False, stop=stop)

        class Rounds:

            def __init__(self, name, rows, into, source, width):
                self.rows, self.source, self.width = rows, source, width
                self.index, self.column = sb(name + "_index", [128, 1], I32, into), sb(name + "_column", [128, 1], F32, into)
                self.gathers = sem(name + "_gathers")
                self.table, self.summed, self.chain = sem(name + "_table"), sem(name + "_summed"), sem(name + "_chain")
                self.added, self.high, self.done = sem(name + "_added"), sem(name + "_high"), sem(name + "_done")

            def each(self, engine, rounds, w, body):
                with engine.If(rounds > 0):
                    with engine.Fori(0, rounds) as k:
                        body(w * rounds + k, k + 1)

            def on_gpsimd(self, pool, rounds, w, first_done):
                last_row = pool.to_reg(N - 1)

                def body(n, k):
                    pool.wait_ge(*first_done)
                    pool.wait_ge(self.done, KC * n)
                    with nc.allow_non_contiguous_dma(reason="one value to a partition"):
                        pool.dma_start(self.index[:, :], slot_src_dram[k, :, bass.ds(w, 1)]).then_inc(self.table, 16)
                        pool.dma_start(self.column[:, :], slot_col_dram[k, :, bass.ds(w, 1)])\
                            .then_inc(self.table, 16)
                    pool.wait_ge(self.table, 32 * (n + 1))
                    pool.sem_inc(self.gathers, 1)
                    pool.indirect_dma_start(self.rows.x[:, 0:self.width], None, self.source,
                                            bass.IndirectOffsetOnAxis(self.index[:, :], 0),
                                            bounds_check=last_row, oob_is_err=False).then_inc(self.rows.gathered, 16)
                self.each(pool, rounds, w, body)

            def on_vector(self, dve, rounds, w, banks, hi, lo):
                def body(n, k):
                    self.rows.on_vector(dve, n, self.column[:, :])
                    for c in range(KC):
                        bank = banks[c % len(banks)][:, 0:BN]
                        dve.wait_ge(self.summed, KC * n + c + 1)
                        Chain(dve, self.chain, KC * n + c).link(
                            dve.tensor_tensor(bank, bank, lo[:, c, :].bitcast(F32), ALU.add))
                        dve.tensor_tensor(bank, bank, hi[:, c, :].bitcast(F32), ALU.add).then_inc(self.added, 1)
                        dve.wait_ge(self.high, KC * n + c + 1)
                        dve.tensor_tensor(lo[:, c, :], bank, hi[:, c, :].bitcast(F32), ALU.subtract)\
                            .then_inc(self.done, 1)
                self.each(dve, rounds, w, body)

            def on_scalar(self, act, rounds, w, banks, hi):
                def body(n, k):
                    self.rows.on_scalar(act, n)
                    for c in range(KC):
                        act.wait_ge(self.added, KC * n + c + 1)
                        act.activation(hi[:, c, :], banks[c % len(banks)][:, 0:BN], ACT.Copy).then_inc(self.high, 1)
                self.each(act, rounds, w, body)

            def on_tensor(self, pe, rounds, w, banks):
                def body(n, k):
                    pe.wait_ge(self.rows.ready, n + 1)
                    for c in range(KC):
                        if c >= len(banks):
                            pe.wait_ge(self.done, KC * n + c + 1 - len(banks))
                        pe.matmul(banks[c % len(banks)][:, 0:BN], self.rows.xr[:, c * 128:(c + 1) * 128],
                                  self.rows.select[:, :], start=True, stop=True).then_inc(self.summed, 1)
                    pe.wait_ge(self.done, KC * (n + 1))
                self.each(pe, rounds, w, body)

        def load_rounds(engine):
            return engine.value_load(rounds_sb[0:1, 0:1], min_val=0, max_val=MAXR - 1)

        with layer0:
            h = sb("h0", [P, J, D], F32, layer0)
            res = sb("res0", [P, J, XW], F32, layer0)
            ht = sb("ht0", [128, KC, BN], F32, layer0)
            g_hi = [sb(f"g_hi{i}", [128, KC, BN], F32R, layer0) for i in range(R)]
            g_lo = [sb(f"g_lo{i}", [128, KC, BN], F32R, layer0) for i in range(R)]
            hid_hi = [sb(f"hid_hi{i}", [128, BN], F32R, layer0) for i in range(2)]
            hid_lo = [sb(f"hid_lo{i}", [128, BN], F32R, layer0) for i in range(2)]
            index = sb("index0", [128, 1], I32, layer0)
            rows = Rows("rows0", layer0, 0)
            nodes = Nodes("nodes0", layer0, 0)
            more = Rounds("more0", Rows("more_rows0", layer0, 0, rows), layer0, x, D)
            out_bank = [layer0.enter_context(nc.psum_tensor(f"out_bank{j}", [128, 512], F32)) for j in range(J)]
            hid_bank = [layer0.enter_context(nc.psum_tensor(f"hid_bank{i}", [128, 512], F32)) for i in range(2)]
            sum_bank = [layer0.enter_context(nc.psum_tensor(f"sum_bank{i}", [128, 512], F32)) for i in range(2)]

            x_in, res_in, stored, cleared = sem("x_in"), sem("res_in"), sem("stored"), sem("cleared")
            indexed, gathers = sem("indexed"), sem("gathers")
            t_done, t_copied = sem("t_done"), sem("t_copied")
            self_high, self_ready, self_done = sem("self_high"), sem("self_ready"), sem("self_done")
            agg_done, agg_added = sem("agg_done"), sem("agg_added")
            g_high, g_ready = sem("g_high"), sem("g_ready")
            z_done, z_relued, z_high, hid_ready = (
                sem("z_done"), sem("z_relued"), sem("z_high"), sem("hid_ready"))
            c_done, evacuated, biased = sem("c_done"), sem("evacuated"), sem("biased")

            with nc.Block() as block:
                @block.sync
                def _(sp):
                    def load(to, b, signal):
                        for p0, p1 in PARTS:
                            sp.dma_start(to[p0:p1, :, 0:D], x_blocks[b, p0:p1, :, :]).then_inc(signal, 16)

                    def store(b):
                        sp.wait_ge(evacuated, J * (b + 1) + J)
                        for p0, p1 in PARTS:
                            sp.dma_start(mid_blocks[b, p0:p1, :, :], res[p0:p1, :, :]).then_inc(stored, 16)
                        sp.wait_ge(stored, 32 * (b + 1))

                    load(h, 0, x_in)
                    sp.wait_ge(cleared, 1)
                    load(res, 0, res_in)
                    with sp.Fori(0, NB - 1) as b:
                        sp.wait_ge(t_done, 2 * (b + 1))
                        load(h, b + 1, x_in)
                        store(b)
                        load(res, b + 1, res_in)
                    store(NB - 1)

                @block.gpsimd
                def _(pool):
                    rounds = load_rounds(pool)
                    last_row = pool.to_reg(N - 1)
                    pool.memset(rows.x[:, :], 0.0).then_inc(indexed, 1)
                    pool.memset(res[:, :, :], 0.0).then_inc(cleared, 1)
                    with pool.Fori(0, W) as w:
                        pool.wait_ge(rows.ready, w)
                        pool.wait_ge(more.done, KC * (rounds * w))
                        pool.wait_ge(indexed, w + 1)
                        pool.tensor_copy(index[:, :], slot_src[:, bass.ds(w, 1)]).then_inc(indexed, 1)
                        pool.wait_ge(indexed, w + 2)
                        pool.sem_inc(gathers, 1)
                        pool.indirect_dma_start(rows.x[:, 0:D], None, x, bass.IndirectOffsetOnAxis(index[:, :], 0),
                                                bounds_check=last_row, oob_is_err=False).then_inc(rows.gathered, 16)
                        more.on_gpsimd(pool, rounds, w, (g_ready, KC * (w + 1)))

                @block.scalar
                def _(act):
                    rounds = load_rounds(act)

                    def transposed(b, half, free):
                        for c in (2 * half, 2 * half + 1):
                            act.wait_ge(t_done, 2 * b + half + 1)
                            act.wait_ge(agg_added, KC * R * b)
                            act.activation(ht[:, c, :], sum_bank[c % 2][:, 0:BN], ACT.Copy).then_inc(t_copied, 1)
                        if free:
                            act.wait_ge(*free)
                        for c in (2 * half, 2 * half + 1):
                            act.wait_ge(t_copied, KC * b + 2 * half + 2)
                            act.activation(g_hi[1][:, c, :], ht[:, c, :], ACT.Copy).then_inc(self_high, 1)

                    def summed(w, r, half, free):
                        if free:
                            act.wait_ge(*free)
                        for c in (2 * half, 2 * half + 1):
                            act.wait_ge(agg_added, KC * w + c + 1)
                            act.activation(g_hi[r][:, c, :], sum_bank[c % 2][:, 0:BN], ACT.Copy).then_inc(g_high, 1)

                    def hidden(b, s):
                        n = STEPS * b + s
                        z = hid_bank[s % 2][:, 0:BN]
                        act.wait_ge(z_done, n + 1)
                        act.activation(z, z, ACT.Relu, bias=b1_col[:, s:s + 1]).then_inc(z_relued, 1)
                        act.wait_ge(z_relued, n + 1)
                        act.wait_ge(c_done, J * (n + 1))
                        act.activation(hid_hi[s % 2][:, :], z, ACT.Copy).then_inc(z_high, 1)

                    def body(b, more_blocks):
                        hidden(b, 0)
                        rows.on_scalar(act, R * b + 1)
                        hidden(b, 1)
                        summed(R * b + 1, 1, 0, (self_done, b + 1))
                        hidden(b, 2)
                        summed(R * b + 1, 1, 1, None)
                        more.on_scalar(act, rounds, R * b + 1, sum_bank, g_hi[1])
                        rows.on_scalar(act, R * b + 2)
                        hidden(b, 3)
                        hidden(b, 4)
                        summed(R * b + 2, 2, 0, (z_done, STEPS * b))
                        hidden(b, 5)
                        summed(R * b + 2, 2, 1, None)
                        more.on_scalar(act, rounds, R * b + 2, sum_bank, g_hi[2])
                        if more_blocks:
                            nodes.on_scalar(act, b + 1, h, h)
                            rows.on_scalar(act, R * (b + 1))
                        for s in (6, 7, 8):
                            hidden(b, s)
                        if more_blocks:
                            transposed(b + 1, 0, (z_done, STEPS * b + 2 * KC))
                        hidden(b, 9)
                        if more_blocks:
                            transposed(b + 1, 1, None)
                        hidden(b, 10)
                        if more_blocks:
                            summed(R * (b + 1), 0, 0, (z_done, STEPS * b + KC))
                        hidden(b, 11)
                        if more_blocks:
                            summed(R * (b + 1), 0, 1, None)
                            more.on_scalar(act, rounds, R * (b + 1), sum_bank, g_hi[0])

                    act.wait_ge(x_in, 32)
                    nodes.on_scalar(act, 0, h, h)
                    rows.on_scalar(act, 0)
                    transposed(0, 0, None)
                    transposed(0, 1, None)
                    summed(0, 0, 0, None)
                    summed(0, 0, 1, None)
                    more.on_scalar(act, rounds, 0, sum_bank, g_hi[0])
                    with act.Fori(0, NB - 1) as b:
                        body(b, True)
                    body(NB - 1, False)

                @block.vector
                def _(dve):
                    rounds = load_rounds(dve)

                    def own(b):
                        dve.wait_ge(x_in, 32 * (b + 1))
                        nodes.on_vector(dve, b, h)

                    def transposed(b, half):
                        for c in (2 * half, 2 * half + 1):
                            dve.wait_ge(self_high, KC * b + c + 1)
                            dve.tensor_tensor(g_lo[1][:, c, :], ht[:, c, :], g_hi[1][:, c, :].bitcast(F32), ALU.subtract)\
                                .then_inc(self_ready, 1)

                    def summed(w, r, half):
                        for c in (2 * half, 2 * half + 1):
                            bank = sum_bank[c % 2][:, 0:BN]
                            dve.wait_ge(agg_done, 2 * w + half + 1)
                            dve.tensor_tensor(bank, bank, ht[:, c, :], ALU.add).then_inc(agg_added, 1)
                        for c in (2 * half, 2 * half + 1):
                            dve.wait_ge(g_high, KC * w + c + 1)
                            dve.tensor_tensor(g_lo[r][:, c, :], sum_bank[c % 2][:, 0:BN],
                                              g_hi[r][:, c, :].bitcast(F32), ALU.subtract).then_inc(g_ready, 1)

                    def hidden(b, s):
                        n = STEPS * b + s
                        dve.wait_ge(z_high, n + 1)
                        dve.tensor_tensor(hid_lo[s % 2][:, :], hid_bank[s % 2][:, 0:BN],
                                          hid_hi[s % 2][:, :].bitcast(F32), ALU.subtract).then_inc(hid_ready, 1)

                    def residual(b):
                        dve.wait_ge(res_in, 32 * (b + 1))
                        dve.tensor_tensor(res[:, :, 0:D], res[:, :, 0:D],
                                          bias[0:P, :].unsqueeze(1).to_broadcast([P, J, D]), ALU.add)
                        dve.tensor_copy(res[:, :, D], dinv[:, bass.ds(J * b, J)]).then_inc(biased, 1)

                    def evacuate(b):
                        dve.wait_ge(biased, b + 1)
                        for j in range(J):
                            dve.wait_ge(c_done, J * (STEPS * b + STEPS + 1) + j + 1)
                            dve.tensor_tensor(res[:, j, 0:D], res[:, j, 0:D], out_bank[j][0:P, :], ALU.add)\
                                .then_inc(evacuated, 1)

                    def gathered(w):
                        dve.wait_ge(agg_done, 2 * w)
                        rows.on_vector(dve, w, slot_col[:, bass.ds(w, 1)])

                    def body(b, more_blocks):
                        hidden(b, 0)
                        gathered(R * b + 1)
                        hidden(b, 1)
                        summed(R * b + 1, 1, 0)
                        hidden(b, 2)
                        summed(R * b + 1, 1, 1)
                        more.on_vector(dve, rounds, R * b + 1, sum_bank, g_hi[1], g_lo[1])
                        gathered(R * b + 2)
                        hidden(b, 3)
                        hidden(b, 4)
                        summed(R * b + 2, 2, 0)
                        hidden(b, 5)
                        summed(R * b + 2, 2, 1)
                        more.on_vector(dve, rounds, R * b + 2, sum_bank, g_hi[2], g_lo[2])
                        if more_blocks:
                            own(b + 1)
                            gathered(R * (b + 1))
                        residual(b)
                        for s in (6, 7, 8):
                            hidden(b, s)
                        if more_blocks:
                            transposed(b + 1, 0)
                        hidden(b, 9)
                        if more_blocks:
                            transposed(b + 1, 1)
                        hidden(b, 10)
                        if more_blocks:
                            summed(R * (b + 1), 0, 0)
                        hidden(b, 11)
                        if more_blocks:
                            summed(R * (b + 1), 0, 1)
                            more.on_vector(dve, rounds, R * (b + 1), sum_bank, g_hi[0], g_lo[0])
                        evacuate(b)

                    dve.sem_inc(evacuated, J)
                    dve.sem_inc(hid_ready, 2)
                    own(0)
                    gathered(0)
                    transposed(0, 0)
                    transposed(0, 1)
                    summed(0, 0, 0)
                    summed(0, 0, 1)
                    more.on_vector(dve, rounds, 0, sum_bank, g_hi[0], g_lo[0])
                    with dve.Fori(0, NB - 1) as b:
                        body(b, True)
                    body(NB - 1, False)

                @block.tensor
                def _(pe):
                    rounds = load_rounds(pe)

                    def transpose(b, half):
                        pe.wait_ge(nodes.ready, J * (b + 1))
                        if half:
                            pe.wait_ge(t_copied, KC * b + 2)
                        else:
                            pe.wait_ge(g_ready, KC * R * b)
                        for c in (2 * half, 2 * half + 1):
                            for j in range(J):
                                mm = pe.transpose(sum_bank[c % 2][:, j * P:(j + 1) * P],
                                                  h[:, j, c * 128:(c + 1) * 128], ident[0:P, 0:P])
                        mm.then_inc(t_done, 1)

                    def aggregate(w, half, banks_free):
                        pe.wait_ge(rows.ready, w + 1)
                        pe.wait_ge(*banks_free)
                        for c in (2 * half, 2 * half + 1):
                            mm = pe.matmul(sum_bank[c % 2][:, 0:BN], rows.xr[:, c * 128:(c + 1) * 128],
                                           rows.select[:, :], start=True, stop=True)
                        mm.then_inc(agg_done, 1)

                    def first(b, s):
                        r, m = divmod(s, KC)
                        n = STEPS * b + s
                        if m == 0:
                            pe.wait_ge(g_ready, KC * (R * b + r + 1))
                        pe.wait_ge(hid_ready, n + 1)
                        for k in range(KC):
                            at = r * KC + k
                            mm = split_product(pe, hid_bank[s % 2][:, 0:BN],
                                               (w1_hi[:, at, m * 128:(m + 1) * 128], w1_lo[:, at, m * 128:(m + 1) * 128]),
                                               (g_hi[r][:, k, :], g_lo[r][:, k, :]), k == 0, k == KC - 1)
                        mm.then_inc(z_done, 1)

                    def own(b):
                        pe.wait_ge(self_ready, KC * (b + 1))
                        for j in range(J):
                            pe.wait_ge(evacuated, J * b + j + 1)
                            for k in range(KC):
                                mm = split_product(pe, out_bank[j][0:P, :],
                                                   (g_hi[1][:, k, j * P:(j + 1) * P], g_lo[1][:, k, j * P:(j + 1) * P]),
                                                   (ws_hi[:, k, :], ws_lo[:, k, :]), k == 0, False)
                        mm.then_inc(self_done, 1)

                    def second(b, s):
                        n = STEPS * b + s
                        pe.wait_ge(hid_ready, n + 3)
                        for j in range(J):
                            mm = split_product(pe, out_bank[j][0:P, :],
                                               (hid_hi[s % 2][:, j * P:(j + 1) * P], hid_lo[s % 2][:, j * P:(j + 1) * P]),
                                               (w2_hi[:, s, :], w2_lo[:, s, :]), False, s == STEPS - 1)
                            if s == STEPS - 1:
                                mm.then_inc(c_done, 1)
                        if s < STEPS - 1:
                            mm.then_inc(c_done, J)

                    def body(b, more_blocks):
                        w = R * b
                        first(b, 0)
                        own(b)
                        first(b, 1)
                        second(b, 0)
                        aggregate(w + 1, 0, (g_ready, KC * (w + 1)))
                        first(b, 2)
                        second(b, 1)
                        aggregate(w + 1, 1, (g_ready, KC * (w + 1) + 2))
                        more.on_tensor(pe, rounds, w + 1, sum_bank)
                        first(b, 3)
                        second(b, 2)
                        first(b, 4)
                        second(b, 3)
                        aggregate(w + 2, 0, (g_ready, KC * (w + 2)))
                        first(b, 5)
                        second(b, 4)
                        aggregate(w + 2, 1, (g_ready, KC * (w + 2) + 2))
                        more.on_tensor(pe, rounds, w + 2, sum_bank)
                        for s in (6, 7, 8):
                            first(b, s)
                            second(b, s - 1)
                        if more_blocks:
                            transpose(b + 1, 0)
                        first(b, 9)
                        second(b, 8)
                        if more_blocks:
                            transpose(b + 1, 1)
                        first(b, 10)
                        second(b, 9)
                        if more_blocks:
                            aggregate(w + 3, 0, (t_copied, KC * (b + 2)))
                        first(b, 11)
                        second(b, 10)
                        if more_blocks:
                            aggregate(w + 3, 1, (g_ready, KC * (w + 3) + 2))
                            more.on_tensor(pe, rounds, w + 3, sum_bank)
                        second(b, 11)

                    pe.sem_inc(c_done, 2 * J)
                    transpose(0, 0)
                    transpose(0, 1)
                    aggregate(0, 0, (t_copied, KC))
                    aggregate(0, 1, (g_ready, 2))
                    more.on_tensor(pe, rounds, 0, sum_bank)
                    with pe.Fori(0, NB - 1) as b:
                        body(b, True)
                    body(NB - 1, False)

        layer1 = ExitStack()
        with layer1:
            RES, TURN = 4, 4
            stage = sb("fused_stage", [128, KC, D], F32, layer1)
            h = sb("h1", [P, J, D], F32, layer1)
            res = [sb(f"res1_{i}", [P, J, XW], F32, layer1) for i in range(RES)]
            ht = sb("ht1", [128, KC, BN], F32, layer1)
            g_hi = [sb(f"u_hi{i}", [128, KC, BN], F32R, layer1) for i in range(2)]
            g_lo = [sb(f"u_lo{i}", [128, KC, BN], F32R, layer1) for i in range(2)]
            index = [sb(f"index1_{i}", [128, 1], I32, layer1) for i in range(1)]
            rows = Rows("rows1", layer1, 1)
            nodes = Nodes("nodes1", layer1, 1)
            more = Rounds("more1", Rows("more_rows1", layer1, 1, rows), layer1, mid, XW)
            out_bank = [layer1.enter_context(nc.psum_tensor(f"y_bank{j}", [128, 512], F32)) for j in range(J)]
            sum_bank = [layer1.enter_context(nc.psum_tensor(f"u_bank{c}", [128, 512], F32)) for c in range(KC)]

            fused_in, fused_high, fused_ready = sem("fused_in"), sem("fused_high"), sem("fused_ready")
            res_in = [sem(f"mid_in{i}") for i in range(RES)]
            stored = [sem(f"out_stored{i}") for i in range(RES)]
            indexed1, gathers1 = sem("indexed1"), sem("gathers1")
            t_done, t_copied = sem("t_done1"), sem("t_copied1")
            rows_used = sem("rows_used1")
            agg_added, g_high, g_ready = sem("agg_added1"), sem("g_high1"), sem("g_ready1")
            out_done, evacuated, biased = sem("out_done1"), sem("evacuated1"), sem("biased1")

            with nc.Block() as block:
                @block.sync
                def _(sp):
                    def load(b, turn, slot):
                        for p0, p1 in PARTS:
                            sp.dma_start(res[slot][p0:p1, :, :], mid_blocks[b, p0:p1, :, :]).then_inc(res_in[slot], 16)

                    def store(b, turn, slot):
                        sp.wait_ge(evacuated, J * (b + 1) + J)
                        for p0, p1 in PARTS:
                            sp.dma_start(out_blocks[b, p0:p1, :, :], res[slot][p0:p1, :, 0:D])\
                                .then_inc(stored[slot], 16)

                    def refill(b, turn, slot):
                        sp.wait_ge(stored[slot], 32 * (turn + 1))
                        load(b, turn + 1, slot)

                    load(0, 0, 0)
                    sp.dma_start(stage[:, :, :].rearrange("p k n -> p (k n)"), fused_dram).then_inc(fused_in, 16)
                    sp.dma_start(bias[:, :], bias2_dram).then_inc(fused_in, 16)
                    for i in range(1, RES):
                        load(i, 0, i)
                    store(0, 0, 0)
                    with sp.Fori(0, NB // TURN - 1) as t:
                        for i in range(TURN):
                            store(TURN * t + i + 1, t + (i + 1) // TURN, (i + 1) % RES)
                            refill(TURN * t + i + RES, t, i)
                    for i in range(1, TURN):
                        store(NB - TURN + i, NB // TURN - 1, i)
                    for i in range(RES):
                        sp.wait_ge(stored[i], 32 * (NB // TURN))

                @block.gpsimd
                def _(pool):
                    rounds = load_rounds(pool)
                    last_row = pool.to_reg(N - 1)
                    pool.memset(rows.x[:, :], 0.0).then_inc(indexed1, 1)

                    def gather(w, first):
                        pool.wait_ge(rows.ready, w)
                        pool.wait_ge(more.done, KC * (rounds * first))
                        pool.wait_ge(indexed1, w + 1)
                        pool.tensor_copy(index[0][:, :], slot_src[:, bass.ds(w, 1)]).then_inc(indexed1, 1)
                        pool.wait_ge(indexed1, w + 2)
                        pool.sem_inc(gathers1, 1)
                        pool.indirect_dma_start(rows.x[:, :], None, mid, bass.IndirectOffsetOnAxis(index[0][:, :], 0),
                                                bounds_check=last_row, oob_is_err=False).then_inc(rows.gathered, 16)

                    with pool.Fori(0, NB) as b:
                        for r in range(R):
                            gather(R * b + r, R * b)
                        for r in range(R):
                            more.on_gpsimd(pool, rounds, R * b + r, (g_ready, KC * (b + 1)))

                @block.scalar
                def _(act):
                    rounds = load_rounds(act)

                    def prepare(b, i):
                        nodes.on_scalar(act, b, res[i % RES], h)
                        for c in range(KC):
                            act.wait_ge(t_done, KC * b + c + 1)
                            act.wait_ge(agg_added, KC * b)
                            act.activation(ht[:, c, :], sum_bank[c][:, 0:BN], ACT.Copy).then_inc(t_copied, 1)
                        for r in range(R):
                            rows.on_scalar(act, R * b + r)
                        for c in range(KC):
                            act.wait_ge(agg_added, KC * b + c + 1)
                            act.activation(g_hi[i % 2][:, c, :], sum_bank[c][:, 0:BN], ACT.Copy).then_inc(g_high, 1)
                        for r in range(R):
                            more.on_scalar(act, rounds, R * b + r, sum_bank, g_hi[i % 2])

                    prepare(0, 0)
                    act.wait_ge(fused_in, 32)
                    act.activation(ws_hi[:, :, :], stage[:, :, :], ACT.Copy).then_inc(fused_high, 1)
                    with act.Fori(0, NB // TURN - 1) as t:
                        for i in range(TURN):
                            act.wait_ge(out_done, J * (TURN * t + i))
                            prepare(TURN * t + i + 1, i + 1)
                    for i in range(TURN - 1):
                        act.wait_ge(out_done, J * (NB - TURN + i))
                        prepare(NB - TURN + i + 1, i + 1)

                @block.vector
                def _(dve):
                    rounds = load_rounds(dve)

                    def prepare(b, turn, i):
                        slot = i % RES
                        dve.wait_ge(res_in[slot], 32 * (turn + 1))
                        nodes.on_vector(dve, b, res[slot])
                        for r in range(R):
                            dve.wait_ge(rows_used, R * b + r)
                            rows.on_vector(dve, R * b + r, slot_col[:, bass.ds(R * b + r, 1)])
                        dve.wait_ge(nodes.ready, J * (b + 1))
                        dve.tensor_tensor(res[slot][:, :, 0:D], res[slot][:, :, 0:D],
                                          bias[0:P, :].unsqueeze(1).to_broadcast([P, J, D]), ALU.add)\
                            .then_inc(biased, 1)
                        for c in range(KC):
                            bank = sum_bank[c][:, 0:BN]
                            dve.wait_ge(rows_used, R * (b + 1))
                            dve.tensor_tensor(bank, bank, ht[:, c, :], ALU.add).then_inc(agg_added, 1)
                        for c in range(KC):
                            dve.wait_ge(g_high, KC * b + c + 1)
                            dve.tensor_tensor(g_lo[i % 2][:, c, :], sum_bank[c][:, 0:BN],
                                              g_hi[i % 2][:, c, :].bitcast(F32), ALU.subtract).then_inc(g_ready, 1)
                        for r in range(R):
                            more.on_vector(dve, rounds, R * b + r, sum_bank, g_hi[i % 2], g_lo[i % 2])

                    def evacuate(b, i):
                        dve.wait_ge(biased, b + 1)
                        for j in range(J):
                            to = res[i % RES]
                            dve.wait_ge(out_done, J * b + j + 1)
                            dve.scalar_tensor_tensor(to[:, j, 0:D], out_bank[j][0:P, :], to[:, j, D:D + 1],
                                                     to[:, j, 0:D], ALU.mult, ALU.add).then_inc(evacuated, 1)

                    dve.sem_inc(evacuated, J)
                    dve.wait_ge(fused_in, 32)
                    prepare(0, 0, 0)
                    dve.wait_ge(fused_high, 1)
                    dve.tensor_tensor(ws_lo[:, :, :], stage[:, :, :], ws_hi[:, :, :].bitcast(F32), ALU.subtract)\
                        .then_inc(fused_ready, 1)
                    with dve.Fori(0, NB // TURN - 1) as t:
                        for i in range(TURN):
                            prepare(TURN * t + i + 1, t + (i + 1) // TURN, i + 1)
                            evacuate(TURN * t + i, i)
                    for i in range(TURN):
                        if i < TURN - 1:
                            prepare(NB - TURN + i + 1, NB // TURN - 1, i + 1)
                        evacuate(NB - TURN + i, i)

                @block.tensor
                def _(pe):
                    rounds = load_rounds(pe)

                    def prepare(b):
                        pe.wait_ge(nodes.ready, J * (b + 1))
                        pe.wait_ge(g_ready, KC * b)
                        for c in range(KC):
                            for j in range(J):
                                mm = pe.transpose(sum_bank[c][:, j * P:(j + 1) * P],
                                                  h[:, j, c * 128:(c + 1) * 128], ident[0:P, 0:P])
                            mm.then_inc(t_done, 1)
                        for r in range(R):
                            pe.wait_ge(rows.ready, R * b + r + 1)
                            for c in range(KC):
                                if r == 0:
                                    pe.wait_ge(t_copied, KC * b + c + 1)
                                mm = pe.matmul(sum_bank[c][:, 0:BN], rows.xr[:, c * 128:(c + 1) * 128],
                                               rows.select[:, :], start=(r == 0), stop=(r == R - 1))
                            mm.then_inc(rows_used, 1)
                        for r in range(R):
                            more.on_tensor(pe, rounds, R * b + r, sum_bank)

                    def multiply(b, i):
                        pe.wait_ge(g_ready, KC * (b + 1))
                        for j in range(J):
                            pe.wait_ge(evacuated, J * b + j + 1)
                            for k in range(KC):
                                mm = split_product(pe, out_bank[j][0:P, :],
                                                   (g_hi[i % 2][:, k, j * P:(j + 1) * P],
                                                    g_lo[i % 2][:, k, j * P:(j + 1) * P]),
                                                   (ws_hi[:, k, :], ws_lo[:, k, :]), k == 0, k == KC - 1)
                            mm.then_inc(out_done, 1)

                    prepare(0)
                    pe.wait_ge(fused_ready, 1)
                    with pe.Fori(0, NB // TURN - 1) as t:
                        for i in range(TURN):
                            prepare(TURN * t + i + 1)
                            multiply(TURN * t + i, i)
                    for i in range(TURN):
                        if i < TURN - 1:
                            prepare(NB - TURN + i + 1)
                        multiply(NB - TURN + i, i)


_INS = ['x', 'src', 'dst', 'edge_type_3', 'L0_gnn_W_self', 'L0_gnn_b_self', 'L0_gnn_W1', 'L0_gnn_b1',
        'L0_gnn_W2', 'L0_gnn_b2', 'L1_gnn_W_gcn', 'L1_gnn_b_gcn', 'L1_gnn_W_dense', 'L1_gnn_b_dense']


def kernel(**inputs):
    import numpy as np
    import concourse.bacc as bacc
    from concourse.bass_utils import run_bass_kernel_spmd

    nc = bacc.Bacc("TRN2", target_bir_lowering=False, num_devices=1)
    arrays = {f"in_{name}": np.ascontiguousarray(inputs[name]) for name in _INS}
    args = [nc.dram_tensor(name, a.shape, mybir.dt.from_np(a.dtype), kind="ExternalInput").ap()
            for name, a in arrays.items()]
    out = nc.dram_tensor("out", arrays["in_x"].shape, mybir.dt.float32, kind="ExternalOutput").ap()
    build_program(nc, *args, out)
    return run_bass_kernel_spmd(nc, [arrays], core_ids=[0]).results[0]["out"]
```

```python
from contextlib import ExitStack

import concourse.bass as bass
from concourse import mybir


def build_program(nc, x, src, dst, edge_type, w_self, b_self, w1, b1, w2, b2, w_gcn, b_gcn, w_dense, b_dense, out):
    F32, F32R, BF16, I32 = mybir.dt.float32, mybir.dt.float32r, mybir.dt.bfloat16, mybir.dt.int32
    ALU, ACT, AX = mybir.AluOpType, mybir.ActivationFunctionType, mybir.AxisListType

    N, D = x.shape
    E = src.shape[0]
    R = w1.shape[0]
    P, J = 125, 4
    BN = P * J
    NB = N // BN
    KC = D // 128
    W = NB * R
    EJ = E // P
    SLOTS = 64
    MAXR = -(-E // SLOTS)
    XW = D + 4
    DINV, SCALE, SHIFT = D, D + 1, D + 2
    EPS = 1e-5
    ROUND = 12582912.0
    ABSENT = 20000.0
    STEPS = R * KC
    assert NB * BN == N and KC * 128 == D and EJ * P == E
    PARTS = ((0, 112), (112, P))

    x_blocks = x.rearrange("(b p j) d -> b p j d", p=P, j=J)
    out_blocks = out.rearrange("(b p j) d -> b p j d", p=P, j=J)
    mid = nc.dram_tensor("mid", [N, XW], F32, kind="Internal").ap()
    mid_blocks = mid.rearrange("(b p j) d -> b p j d", p=P, j=J)
    sent = nc.dram_tensor("sent", [N, D], F32, kind="Internal").ap()
    sent_blocks = sent.rearrange("(b p j) d -> b p j d", p=P, j=J)
    fused_dram = nc.dram_tensor("fused_w", [128, KC * D], F32, kind="Internal").ap()
    bias2_dram = nc.dram_tensor("bias2", [128, D], F32, kind="Internal").ap()
    slot_src_dram = nc.dram_tensor("slot_src", [MAXR, 128, W], I32, kind="Internal").ap()
    slot_col_dram = nc.dram_tensor("slot_col", [MAXR, 128, W], F32, kind="Internal").ap()

    class Chain:

        def __init__(self, engine, sem, at=0):
            self.engine, self.sem, self.at, self.n = engine, sem, at, 0

        def link(self, instruction):
            self.n += 1
            instruction.then_inc(self.sem, 1)
            self.engine.wait_ge(self.sem, self.at + self.n)

    with ExitStack() as ctx:
        def sb(name, shape, dt=F32, into=ctx):
            return into.enter_context(nc.sbuf_tensor(name, shape, dt))

        def sem(name):
            return ctx.enter_context(nc.semaphore(name))

        ws_hi, ws_lo = sb("ws_hi", [128, KC, D], F32R), sb("ws_lo", [128, KC, D], F32R)
        bias = sb("bias", [128, D])
        b1_col = sb("b1_col", [128, STEPS])
        ident = sb("ident", [128, 128])
        node_iota = sb("node_iota", [128, BN])
        dinv = sb("dinv", [P, NB * J])
        slot_src = sb("slot_src_sb", [128, W], I32)
        slot_col = sb("slot_col_sb", [128, W])
        rounds_sb = sb("rounds_sb", [128, 1], I32)

        layer0 = ExitStack()
        w1_hi, w1_lo = sb("w1_hi", [128, R * KC, D], F32R, layer0), sb("w1_lo", [128, R * KC, D], F32R, layer0)
        w2_hi, w2_lo = sb("w2_hi", [128, R * KC, D], F32R, layer0), sb("w2_lo", [128, R * KC, D], F32R, layer0)

        prep = ExitStack()
        with prep:
            def tmp(name, shape, dt=F32):
                return sb(name, shape, dt, prep)

            stage = [tmp(f"stage{i}", [128, KC, D]) for i in range(2)]
            gcn, gcn_t, dense = tmp("gcn", [128, KC, D]), tmp("gcn_t", [128, KC, D]), tmp("dense", [128, KC, D])
            ints = tmp("ints", [P, 3, EJ], I32)
            srcf, dstf, typef = (tmp(n, [P, EJ]) for n in ("srcf", "dstf", "typef"))
            blk, loc, prt, row4, col, bucket, qidx, rank = (
                tmp(n, [P, EJ]) for n in ("blk", "loc", "prt", "row4", "col", "bucket", "qidx", "rank"))
            hot = tmp("hot", [P, EJ, W])
            before = tmp("before", [P, EJ, W])
            pairs = tmp("pairs", [P, EJ, 2, W])
            pick = tmp("pick", [P, EJ, 128])
            hot_p, hot_q = tmp("hot_p", [P, EJ, P], BF16), tmp("hot_q", [P, EJ, NB * J], BF16)
            row_sum = tmp("row_sum", [P, W])
            iota_w, iota_p, iota_q, iota_s = (
                tmp(n, [P, k]) for n, k in (("iota_w", W), ("iota_p", P), ("iota_q", NB * J), ("iota_s", 128)))
            tri = tmp("tri", [P, P])
            ones = tmp("ones", [P, 128])
            b1_rows, bg_rows = tmp("b1_rows", [STEPS, 128]), tmp("bg_rows", [KC, 128])
            bg_col = tmp("bg_col", [128, KC])
            bias_rows, dense_row = tmp("bias_rows", [R + 1, D]), tmp("dense_row", [1, D])
            bias2 = tmp("bias2_sb", [128, D])
            deg, root, y2 = tmp("deg", [P, NB * J]), tmp("root", [P, NB * J]), tmp("y2", [P, NB * J])
            top = tmp("top", [128, 2])
            empty = tmp("empty", [128, W])
            psum = ExitStack()
            with psum:
                def pb(name, shape):
                    return psum.enter_context(nc.psum_tensor(name, shape, F32))

                p_rank, p_count, p_slots, p_deg, p_cols = (
                    pb(n, [128, 512]) for n in ("p_rank", "p_count", "p_slots", "p_deg", "p_cols"))
                p_fuse = [pb(f"p_fuse{i}", [128, 512]) for i in range(3)]

                edges_in, consts, w_in = sem("edges_in"), sem("consts"), [sem("w_in0"), sem("w_in1")]
                fuse_in, bias_in = sem("fuse_in"), sem("bias_in")
                chain_p, chain_g = sem("chain_p"), sem("chain_g")
                w_high, w_split = sem("w_high"), sem("w_split")
                sums_ready, ranks_up, picked, slots_up = (
                    sem("sums_ready"), sem("ranks_up"), sem("picked"), sem("slots_up"))
                slots_out, slots_stored, slots_back, tables_free = (
                    sem("slots_out"), sem("slots_stored"), sem("slots_back"), sem("tables_free"))
                hots_ready, deg_up, deg_ready, root_ready = (
                    sem("hots_ready"), sem("deg_up"), sem("deg_ready"), sem("root_ready"))
                rounds_ready = sem("rounds_ready")
                cols_up, cols_copied = sem("cols_up"), sem("cols_copied")
                gt_up, gt_copied, fused_up, fused_copied, fused_out = (
                    sem("gt_up"), sem("gt_copied"), sem("fused_up"), sem("fused_copied"), sem("fused_out"))
                bias_up, bias2_up, bias2_copied = sem("bias_up"), sem("bias2_up"), sem("bias2_copied")

                weights = ([(w_self, ws_hi, ws_lo, 0)] + [(w1[r], w1_hi, w1_lo, r * KC) for r in range(R)]
                           + [(w2[r], w2_hi, w2_lo, r * KC) for r in range(R)])

                with nc.Block() as block:
                    @block.sync
                    def _(sp):
                        for i, a in enumerate((dst, edge_type, src)):
                            sp.dma_start(ints[:, i, :], a.rearrange("(p i) -> p i", p=P)).then_inc(edges_in, 16)
                        for i, (w, _, _, _) in enumerate(weights):
                            if i >= 2:
                                sp.wait_ge(w_split, i - 1)
                            sp.dma_start(stage[i % 2][:, :, :], w.rearrange("(k p) n -> p k n", p=128))\
                                .then_inc(w_in[i % 2], 16)
                        sp.wait_ge(rounds_ready, 1)
                        rounds = sp.value_load(rounds_sb[0:1, 0:1], min_val=0, max_val=MAXR - 1)
                        sp.wait_ge(slots_stored, 32 * (rounds + 1))
                        sp.dma_start(slot_src[:, :], slot_src_dram[0]).then_inc(slots_back, 16)
                        sp.dma_start(slot_col[:, :], slot_col_dram[0]).then_inc(slots_back, 16)
                        sp.wait_ge(slots_back, 32)
                        sp.wait_ge(fused_copied, KC)
                        sp.dma_start(fused_dram, gcn[:, :, :].rearrange("p k n -> p (k n)")).then_inc(fused_out, 16)
                        sp.wait_ge(bias2_copied, 1)
                        sp.dma_start(bias2_dram, bias2[:, :]).then_inc(fused_out, 16)
                        sp.wait_ge(fused_out, 32)

                    @block.gpsimd
                    def _(pool):
                        link = Chain(pool, chain_g).link
                        for t, k in ((iota_w, W), (iota_p, P), (iota_q, NB * J)):
                            pool.iota(t[:, :], [[1, k]], base=0, channel_multiplier=0,
                                      allow_small_or_imprecise_dtypes=True)
                        pool.iota(iota_s[:, :].rearrange("p (a s) -> p a s", a=2), [[0, 2], [1, SLOTS]], base=0,
                                  channel_multiplier=0, allow_small_or_imprecise_dtypes=True)
                        pool.iota(node_iota[:, :], [[1, BN]], base=0, channel_multiplier=0,
                                  allow_small_or_imprecise_dtypes=True)
                        pool.memset(ones[:, :], 1.0)
                        pool.memset(tri[:, :], 1.0)
                        link(pool.memset(ident[:, :], 0.0))
                        link(pool.affine_select(out=ident[:, :], in_=ident[:, :], compare_op=ALU.not_equal, fill=1.0,
                                                base=0, pattern=[[-1, 128]], channel_multiplier=1))
                        pool.affine_select(out=tri[:, :], in_=tri[:, :], compare_op=ALU.is_ge, fill=0.0,
                                           base=-1, pattern=[[1, P]], channel_multiplier=-1).then_inc(consts, 1)
                        pool.wait_ge(rounds_ready, 1)
                        rounds = pool.value_load(rounds_sb[0:1, 0:1], min_val=0, max_val=MAXR - 1)
                        with pool.Fori(0, rounds + 1) as k:
                            pool.wait_ge(slots_out, 4 * (k + 1))
                            pool.dma_start(slot_src_dram[k], slot_src[:, :]).then_inc(slots_stored, 16)
                            pool.dma_start(slot_col_dram[k], slot_col[:, :]).then_inc(slots_stored, 16)
                            pool.wait_ge(slots_stored, 32 * (k + 1))
                            pool.sem_inc(tables_free, 1)

                    @block.scalar
                    def _(act):
                        act.dma_start(gcn[:, :, :], w_gcn.rearrange("(k p) n -> p k n", p=128)).then_inc(fuse_in, 16)
                        act.dma_start(dense[:, :, :], w_dense.rearrange("(k p) n -> p k n", p=128))\
                            .then_inc(fuse_in, 16)
                        act.dma_start(b1_rows[:, :], b1.rearrange("r (m p) -> (r m) p", p=128)).then_inc(bias_in, 16)
                        act.dma_start(bg_rows[:, :], b_gcn.rearrange("(m p) -> m p", p=128)).then_inc(bias_in, 16)
                        act.dma_start(bias_rows[0:1, :], b_self[None, :]).then_inc(bias_in, 16)
                        act.dma_start(bias_rows[1:R + 1, :], b2).then_inc(bias_in, 16)
                        act.dma_start(dense_row[:, :], b_dense[None, :]).then_inc(bias_in, 16)

                        def high(i):
                            _, hi, _, at = weights[i]
                            act.wait_ge(w_in[i % 2], 16 * (i // 2 + 1))
                            act.activation(hi[:, at:at + KC, :], stage[i % 2][:, :, :], ACT.Copy).then_inc(w_high, 1)

                        high(0)
                        act.wait_ge(deg_ready, 1)
                        act.activation(root[:, :], deg[:, :], ACT.Sqrt).then_inc(root_ready, 1)
                        high(1)
                        for k in range(KC):
                            act.wait_ge(gt_up, k + 1)
                            act.activation(gcn_t[:, k, :], p_fuse[k % 2][:, :], ACT.Copy).then_inc(gt_copied, 1)
                        high(2)
                        for m in range(KC):
                            act.wait_ge(fused_up, m + 1)
                            act.activation(gcn[:, m, :], p_fuse[m % 2][:, :], ACT.Copy).then_inc(fused_copied, 1)
                        for i in range(3, len(weights)):
                            high(i)

                    @block.vector
                    def _(dve):
                        link = Chain(dve, chain_p).link

                        def low(i):
                            _, hi, lo, at = weights[i]
                            dve.wait_ge(w_high, i + 1)
                            dve.tensor_tensor(lo[:, at:at + KC, :], stage[i % 2][:, :, :],
                                              hi[:, at:at + KC, :].bitcast(F32), ALU.subtract).then_inc(w_split, 1)

                        def floor_div(to, scratch, a, by, mid_point):
                            link(dve.tensor_scalar(scratch[:, :], a[:, :], mid_point, 1.0 / by, ALU.subtract, ALU.mult))
                            link(dve.tensor_scalar(to[:, :], scratch[:, :], ROUND, ROUND, ALU.add, ALU.subtract))

                        def fma(to, a, by, plus):
                            link(dve.scalar_tensor_tensor(to[:, :], a[:, :], by, plus[:, :], ALU.mult, ALU.add))

                        dve.wait_ge(edges_in, 48)
                        dve.tensor_copy(dstf[:, :], ints[:, 0, :])
                        dve.tensor_copy(typef[:, :], ints[:, 1, :])
                        link(dve.tensor_copy(srcf[:, :], ints[:, 2, :]))
                        floor_div(blk, rank, dstf, BN, (BN - 1) / 2)
                        fma(loc, blk, -float(BN), dstf)
                        floor_div(prt, rank, loc, J, (J - 1) / 2)
                        fma(row4, prt, -float(J), loc)
                        fma(col, row4, float(P), prt)
                        fma(bucket, blk, float(R), typef)
                        fma(qidx, blk, float(J), row4)
                        dve.wait_ge(consts, 1)

                        def one_hot(to, iota, k, a):
                            return dve.tensor_tensor(
                                to[:, :, :], iota[:, :].unsqueeze(1).to_broadcast([P, EJ, k]),
                                a[:, :].unsqueeze(2).to_broadcast([P, EJ, k]), ALU.is_equal)

                        link(one_hot(hot, iota_w, W, bucket))
                        link(dve.memset(before[:, 0, :], 0.0))
                        for i in range(1, EJ):
                            link(dve.tensor_tensor(before[:, i, :], before[:, i - 1, :], hot[:, i - 1, :], ALU.add))
                        dve.tensor_tensor(row_sum[:, :], before[:, EJ - 1, :], hot[:, EJ - 1, :], ALU.add)\
                            .then_inc(sums_ready, 1)
                        one_hot(hot_p, iota_p, P, prt)
                        one_hot(hot_q, iota_q, NB * J, qidx).then_inc(hots_ready, 1)
                        link(dve.scalar_tensor_tensor(
                            pairs[:, :, 0, :], srcf[:, :].unsqueeze(2).to_broadcast([P, EJ, W]), 1.0,
                            hot[:, :, :], ALU.add, ALU.mult))
                        link(dve.scalar_tensor_tensor(
                            pairs[:, :, 1, :], col[:, :].unsqueeze(2).to_broadcast([P, EJ, W]), 1.0,
                            hot[:, :, :], ALU.add, ALU.mult))
                        dve.wait_ge(ranks_up, 1)
                        link(dve.tensor_tensor(before[:, :, :], before[:, :, :],
                                               p_rank[0:P, 0:W].unsqueeze(1).to_broadcast([P, EJ, W]), ALU.add))
                        link(dve.tensor_tensor(before[:, :, :], before[:, :, :], hot[:, :, :], ALU.mult))
                        link(dve.tensor_reduce(rank[:, :], before[:, :, :], AX.X, ALU.add))
                        dve.wait_ge(ranks_up, 2)
                        link(dve.tensor_reduce(top[:, 0:1], p_count[:, 0:W], AX.X, ALU.max))
                        link(dve.tensor_scalar(top[:, 1:2], top[:, 0:1], (SLOTS - 1) / 2, 1.0 / SLOTS,
                                               ALU.add, ALU.mult))
                        link(dve.tensor_scalar(top[:, 0:1], top[:, 1:2], ROUND, ROUND, ALU.add, ALU.subtract))
                        dve.tensor_scalar(rounds_sb[:, :], top[:, 0:1], -1.0, 0.0, ALU.add, ALU.max).then_inc(rounds_ready, 1)
                        dve.wait_ge(deg_up, 1)
                        dve.tensor_scalar(deg[:, :], p_deg[0:P, 0:NB * J], 1.0, None, ALU.add).then_inc(deg_ready, 1)
                        dve.wait_ge(root_ready, 1)
                        link(dve.reciprocal(dinv[:, :], root[:, :]))
                        link(dve.tensor_tensor(y2[:, :], dinv[:, :], dinv[:, :], ALU.mult))
                        link(dve.tensor_tensor(y2[:, :], y2[:, :], deg[:, :], ALU.mult))
                        link(dve.tensor_scalar(y2[:, :], y2[:, :], -0.5, 1.5, ALU.mult, ALU.add))
                        link(dve.tensor_tensor(dinv[:, :], dinv[:, :], y2[:, :], ALU.mult))
                        dve.wait_ge(rounds_ready, 1)
                        rounds = dve.value_load(rounds_sb[0:1, 0:1], min_val=0, max_val=MAXR - 1)
                        dve.sem_inc(tables_free, 1)
                        with dve.Fori(0, rounds + 1) as k:
                            dve.tensor_tensor(pick[:, :, :], iota_s[:, :].unsqueeze(1).to_broadcast([P, EJ, 128]),
                                              rank[:, :].unsqueeze(2).to_broadcast([P, EJ, 128]), ALU.is_equal)\
                                .then_inc(picked, 1)
                            dve.wait_ge(slots_up, k + 1)
                            dve.wait_ge(tables_free, k + 1)
                            inner = Chain(dve, slots_out, 4 * k).link
                            inner(dve.tensor_scalar(empty[:, :], p_slots[:, 0:W], 0.0, ABSENT, ALU.is_equal, ALU.mult))
                            inner(dve.scalar_tensor_tensor(slot_src[:, :], p_slots[:, 0:W], -1.0, empty[:, :],
                                                           ALU.add, ALU.add))
                            inner(dve.tensor_scalar(slot_col[:, :], p_slots[:, W:2 * W], -1.0, None, ALU.add))
                            inner(dve.tensor_scalar(rank[:, :], rank[:, :], -float(SLOTS), None, ALU.add))
                        low(0)
                        dve.wait_ge(cols_up, 1)
                        dve.tensor_copy(b1_col[:, :], p_cols[:, 0:STEPS])
                        dve.tensor_copy(bg_col[:, :], p_cols[:, 16:16 + KC]).then_inc(cols_copied, 1)
                        low(1)
                        dve.wait_ge(bias_up, 1)
                        dve.tensor_copy(bias[:, :], p_count[:, :])
                        low(2)
                        dve.wait_ge(bias2_up, 1)
                        dve.tensor_copy(bias2[:, :], p_fuse[2][:, :]).then_inc(bias2_copied, 1)
                        for i in range(3, len(weights)):
                            low(i)

                    @block.tensor
                    def _(pe):
                        pe.wait_ge(consts, 1)
                        pe.wait_ge(sums_ready, 1)
                        pe.matmul(p_rank[0:P, 0:W], tri[:, :], row_sum[:, :], start=True, stop=True)\
                            .then_inc(ranks_up, 1)
                        pe.matmul(p_count[:, 0:W], ones[:, :], row_sum[:, :], start=True, stop=True)\
                            .then_inc(ranks_up, 1)
                        pe.wait_ge(hots_ready, 1)
                        for i in range(EJ):
                            mm = pe.matmul(p_deg[0:P, 0:NB * J], hot_p[:, i, :], hot_q[:, i, :],
                                           start=(i == 0), stop=(i == EJ - 1))
                        mm.then_inc(deg_up, 1)
                        pe.wait_ge(rounds_ready, 1)
                        rounds = pe.value_load(rounds_sb[0:1, 0:1], min_val=0, max_val=MAXR - 1)
                        with pe.Fori(0, rounds + 1) as k:
                            pe.wait_ge(picked, k + 1)
                            for i in range(EJ):
                                mm = pe.matmul(p_slots[:, 0:2 * W], pick[:, i, :],
                                               pairs[:, i, :, :].rearrange("p a w -> p (a w)"),
                                               start=(i == 0), stop=(i == EJ - 1))
                            mm.then_inc(slots_up, 1)
                        pe.wait_ge(bias_in, 16 * 5)
                        pe.transpose(p_cols[:, 0:STEPS], b1_rows[:, :], ident[0:STEPS, 0:STEPS])
                        pe.transpose(p_cols[:, 16:16 + KC], bg_rows[:, :], ident[0:KC, 0:KC]).then_inc(cols_up, 1)
                        pe.matmul(p_count[:, :], ones[0:R + 1, :], bias_rows[:, :], start=True, stop=True)\
                            .then_inc(bias_up, 1)
                        pe.wait_ge(fuse_in, 32)
                        for k in range(KC):
                            if k >= 2:
                                pe.wait_ge(gt_copied, k - 1)
                            for m in range(KC):
                                mm = pe.transpose(p_fuse[k % 2][:, m * 128:(m + 1) * 128],
                                                  gcn[:, m, k * 128:(k + 1) * 128], ident[:, :])
                            mm.then_inc(gt_up, 1)
                        for m in range(KC):
                            pe.wait_ge(gt_copied, KC)
                            if m >= 2:
                                pe.wait_ge(fused_copied, m - 1)
                            for k in range(KC):
                                mm = pe.matmul(p_fuse[m % 2][:, :], gcn_t[:, k, m * 128:(m + 1) * 128], dense[:, k, :],
                                               start=(k == 0), stop=(k == KC - 1))
                            mm.then_inc(fused_up, 1)
                        pe.wait_ge(cols_copied, 1)
                        for k in range(KC):
                            pe.matmul(p_fuse[2][:, :], bg_col[:, k:k + 1].to_broadcast([128, 128]),
                                      dense[:, k, :], start=(k == 0), stop=False)
                        pe.matmul(p_fuse[2][:, :], ones[0:1, :], dense_row[:, :], start=False, stop=True)\
                            .then_inc(bias2_up, 1)

        class Rows:
            LINKS = 6

            def __init__(self, name, into, norm, share=None):
                self.norm = norm
                if share:
                    self.x, self.xr, self.select, self.small = share.x, share.xr, share.select, share.small
                else:
                    self.x = sb(name + "_x", [128, D], F32, into)
                    self.xr = sb(name + "_xr", [128, D], F32R, into)
                    self.select = sb(name + "_select", [128, BN], F32R, into)
                    self.small = sb(name + "_small", [128, 16], F32, into) if norm else None
                self.gathered = sem(name + "_gathered")
                if norm:
                    self.chain, self.relued = sem(name + "_chain"), sem(name + "_relued")
                    self.var_ready, self.root_ready = sem(name + "_var_ready"), sem(name + "_root_ready")
                    self.norm_ready = sem(name + "_norm_ready")
                self.high_ready, self.ready = sem(name + "_high_ready"), sem(name + "_ready")

            def stats_on_vector(self, dve, n, column):
                if not self.norm:
                    dve.tensor_scalar(self.select[:, :], node_iota[:, :], column, None, ALU.is_equal)
                    return
                link = Chain(dve, self.chain, self.LINKS * n).link
                stat, mean, var = self.small[:, 0:6], self.small[:, 6:7], self.small[:, 7:8]
                v, root, y, t, shift = (self.small[:, i:i + 1] for i in range(8, 13))
                dve.wait_ge(self.gathered, 16 * (n + 1))
                link(dve.bn_stats(stat, self.x[:, :]))
                dve.tensor_scalar(self.select[:, :], node_iota[:, :], column, None, ALU.is_equal)
                link(dve.bn_aggr(self.small[:, 6:8], stat))
                dve.tensor_scalar(v, var, EPS, None, ALU.add).then_inc(self.var_ready, 1)
                dve.wait_ge(self.root_ready, n + 1)
                link(dve.reciprocal(y, root))
                link(dve.scalar_tensor_tensor(t, y, y, v, ALU.mult, ALU.mult))
                link(dve.tensor_scalar(t, t, -0.5, 1.5, ALU.mult, ALU.add))
                link(dve.tensor_tensor(y, y, t, ALU.mult))
                dve.scalar_tensor_tensor(shift, mean, -1.0, y, ALU.mult, ALU.mult).then_inc(self.norm_ready, 1)

            def split_on_vector(self, dve, n):
                dve.wait_ge(self.high_ready, n + 1)
                dve.tensor_tensor(self.xr[SLOTS:128, :], self.x[SLOTS:128, :], self.xr[SLOTS:128, :].bitcast(F32),
                                  ALU.subtract).then_inc(self.ready, 1)

            def stats_on_scalar(self, act, n):
                if self.norm:
                    act.wait_ge(self.var_ready, n + 1)
                    act.activation(self.small[:, 9:10], self.small[:, 8:9], ACT.Sqrt).then_inc(self.root_ready, 1)

            def split_on_scalar(self, act, n):
                if self.norm:
                    act.wait_ge(self.norm_ready, n + 1)
                    act.activation(self.x[:, :], self.x[:, :], ACT.Relu, bias=self.small[:, 12:13],
                                   scale=self.small[:, 10:11]).then_inc(self.relued, 1)
                    act.wait_ge(self.relued, n + 1)
                else:
                    act.wait_ge(self.gathered, 16 * (n + 1))
                act.activation(self.xr[:, :], self.x[:, :], ACT.Copy).then_inc(self.high_ready, 1)

            def on_vector(self, dve, n, column):
                self.stats_on_vector(dve, n, column)
                self.split_on_vector(dve, n)

            def on_scalar(self, act, n):
                self.stats_on_scalar(act, n)
                self.split_on_scalar(act, n)

        class Nodes:
            LINKS = 7

            def __init__(self, name, into, degree):
                self.degree = degree
                self.stat = sb(name + "_stat", [P, J, 6], F32, into)
                self.mean_var = sb(name + "_mean_var", [P, J, 2], F32, into)
                self.v, self.root, self.y, self.t, self.shift = (
                    sb(name + n, [P, J], F32, into) for n in ("_v", "_root", "_y", "_t", "_shift"))
                self.chain, self.var_ready, self.root_ready = (
                    sem(name + "_chain"), sem(name + "_var_ready"), sem(name + "_root_ready"))
                self.norm_ready, self.ready = sem(name + "_norm_ready"), sem(name + "_ready")

            def on_vector(self, dve, b, source):
                link = Chain(dve, self.chain, (self.LINKS + self.degree) * b).link
                for j in range(J):
                    step = dve.bn_stats(self.stat[:, j, :], source[:, j, 0:D])
                link(step)
                dve.memset(self.t[:, :], 0.0)
                for j in range(J):
                    step = dve.bn_aggr(self.mean_var[:, j, :], self.stat[:, j, :])
                link(step)
                dve.tensor_scalar(self.v[:, :], self.mean_var[:, :, 1], EPS, None, ALU.add)\
                    .then_inc(self.var_ready, 1)
                dve.wait_ge(self.root_ready, b + 1)
                y, t = self.y[:, :], self.t[:, :]
                link(dve.reciprocal(y, self.root[:, :]))
                link(dve.tensor_tensor(t, y, y, ALU.mult))
                link(dve.tensor_tensor(t, t, self.v[:, :], ALU.mult))
                link(dve.tensor_scalar(t, t, -0.5, 1.5, ALU.mult, ALU.add))
                link(dve.tensor_tensor(y, y, t, ALU.mult))
                scale, shift = y, self.shift[:, :]
                if self.degree:
                    scale, shift = source[:, :, SCALE], source[:, :, SHIFT]
                    link(dve.tensor_tensor(scale, y, source[:, :, DINV], ALU.mult))
                dve.scalar_tensor_tensor(shift, self.mean_var[:, :, 0], -1.0, scale, ALU.mult, ALU.mult)\
                    .then_inc(self.norm_ready, 1)

            def on_scalar(self, act, b):
                act.wait_ge(self.var_ready, b + 1)
                act.activation(self.root[:, :], self.v[:, :], ACT.Sqrt).then_inc(self.root_ready, 1)
                act.wait_ge(self.norm_ready, b + 1)

        def split_product(pe, bank, stationary, moving, start, stop):
            (s_hi, s_lo), (m_hi, m_lo) = stationary, moving
            pe.matmul(bank, s_hi, m_hi, start=start, stop=False)
            pe.matmul(bank, s_hi, m_lo, start=False, stop=False)
            return pe.matmul(bank, s_lo, m_hi, start=False, stop=stop)

        class Rounds:

            def __init__(self, name, into, source, rows):
                self.source, self.rows = source, rows
                self.index, self.column = sb(name + "_index", [128, 1], I32, into), sb(name + "_column", [128, 1], F32, into)
                self.table, self.gathers, self.chain = sem(name + "_table"), sem(name + "_gathers"), sem(name + "_chain")
                self.summed, self.added = sem(name + "_summed"), sem(name + "_added")
                self.high, self.done = sem(name + "_high"), sem(name + "_done")

            def each(self, engine, rounds, w, body):
                with engine.If(rounds > 0):
                    with engine.Fori(0, rounds) as k:
                        body(w * rounds + k, k + 1)

            def on_gpsimd(self, pool, rounds, w, first_done, last_row):
                def body(n, k):
                    pool.wait_ge(*first_done)
                    pool.wait_ge(self.done, KC * n + 1)
                    with nc.allow_non_contiguous_dma(reason="one value to a partition"):
                        pool.dma_start(self.index[:, :], slot_src_dram[k, :, bass.ds(w, 1)]).then_inc(self.table, 16)
                        pool.dma_start(self.column[:, :], slot_col_dram[k, :, bass.ds(w, 1)])\
                            .then_inc(self.table, 16)
                    pool.wait_ge(self.table, 32 * (n + 1))
                    pool.sem_inc(self.gathers, 1)
                    pool.indirect_dma_start(self.rows.x[:, :], None, self.source,
                                            bass.IndirectOffsetOnAxis(self.index[:, :], 0),
                                            bounds_check=last_row, oob_is_err=False).then_inc(self.rows.gathered, 16)
                self.each(pool, rounds, w, body)

            def on_vector(self, dve, rounds, w, banks, hi, lo):
                def body(n, k):
                    dve.wait_ge(self.rows.gathered, 16 * (n + 1))
                    self.rows.on_vector(dve, n, self.column[:, :])
                    for c in range(KC):
                        bank = banks[c % len(banks)][:, 0:BN]
                        dve.wait_ge(self.summed, KC * n + c + 1)
                        Chain(dve, self.chain, KC * n + c).link(
                            dve.tensor_tensor(bank, bank, lo[:, c, :].bitcast(F32), ALU.add))
                        dve.tensor_tensor(bank, bank, hi[:, c, :].bitcast(F32), ALU.add).then_inc(self.added, 1)
                        dve.wait_ge(self.high, KC * n + c + 1)
                        dve.tensor_tensor(lo[:, c, :], bank, hi[:, c, :].bitcast(F32), ALU.subtract)\
                            .then_inc(self.done, 1)
                self.each(dve, rounds, w, body)

            def on_scalar(self, act, rounds, w, banks, hi):
                def body(n, k):
                    self.rows.on_scalar(act, n)
                    for c in range(KC):
                        act.wait_ge(self.added, KC * n + c + 1)
                        act.activation(hi[:, c, :], banks[c % len(banks)][:, 0:BN], ACT.Copy).then_inc(self.high, 1)
                self.each(act, rounds, w, body)

            def on_tensor(self, pe, rounds, w, banks):
                def body(n, k):
                    pe.wait_ge(self.rows.ready, n + 1)
                    for c in range(KC):
                        if c >= len(banks):
                            pe.wait_ge(self.done, KC * n + c + 1 - len(banks) + 1)
                        pe.matmul(banks[c % len(banks)][:, 0:BN], self.rows.xr[:, c * 128:(c + 1) * 128],
                                  self.rows.select[:, :], start=True, stop=True).then_inc(self.summed, 1)
                    pe.wait_ge(self.done, KC * (n + 1) + 1)
                self.each(pe, rounds, w, body)

        def load_rounds(engine):
            return engine.value_load(rounds_sb[0:1, 0:1], min_val=0, max_val=MAXR - 1)

        with layer0:
            h_wide = sb("h0", [128, J, D], F32, layer0)
            h = h_wide[0:P]
            res = sb("res0", [P, J, XW], F32, layer0)
            ht = sb("ht0", [128, KC, BN], F32, layer0)
            g_hi = [sb(f"g_hi{i}", [128, KC, BN], F32R, layer0) for i in range(R)]
            g_lo = [sb(f"g_lo{i}", [128, KC, BN], F32R, layer0) for i in range(R)]
            hid_hi = [sb(f"hid_hi{i}", [128, BN], F32R, layer0) for i in range(2)]
            hid_lo = [sb(f"hid_lo{i}", [128, BN], F32R, layer0) for i in range(2)]
            index = sb("index0", [128, 1], I32, layer0)
            message = [sb(f"message{i}", [P, D], F32, layer0) for i in range(2)]
            rows = Rows("rows0", layer0, True)
            nodes = Nodes("nodes0", layer0, 0)
            outs = Nodes("outs0", layer0, 1)
            more = Rounds("more0", layer0, x, Rows("more_rows0", layer0, True, rows))
            out_bank = [layer0.enter_context(nc.psum_tensor(f"out_bank{j}", [128, 512], F32)) for j in range(J)]
            hid_bank = [layer0.enter_context(nc.psum_tensor(f"hid_bank{i}", [128, 512], F32)) for i in range(2)]
            sum_bank = [layer0.enter_context(nc.psum_tensor(f"sum_bank{i}", [128, 512], F32)) for i in range(2)]

            m_made, m_stored = sem("m_made"), [sem("m_stored0"), sem("m_stored1")]
            fused_in, fused_high, fused_ready = sem("fused_in"), sem("fused_high"), sem("fused_ready")
            x_in, res_in, stored, cleared = sem("x_in"), sem("res_in"), sem("stored"), sem("cleared")
            indexed, gathers = sem("indexed"), sem("gathers")
            t_done, t_copied = sem("t_done"), sem("t_copied")
            self_high, self_ready, self_done = sem("self_high"), sem("self_ready"), sem("self_done")
            agg_done, agg_added = sem("agg_done"), sem("agg_added")
            g_high, g_ready = sem("g_high"), sem("g_ready")
            z_done, z_relued, z_high, hid_ready = (
                sem("z_done"), sem("z_relued"), sem("z_high"), sem("hid_ready"))
            c_done, evacuated, biased = sem("c_done"), sem("evacuated"), sem("biased")

            with nc.Block() as block:
                @block.sync
                def _(sp):
                    def load(to, b, signal):
                        for p0, p1 in PARTS:
                            sp.dma_start(to[p0:p1, :, 0:D], x_blocks[b, p0:p1, :, :]).then_inc(signal, 16)

                    def store(b):
                        for j in range(J):
                            sp.wait_ge(m_made, J * b + j + 1)
                            for p0, p1 in PARTS:
                                sp.dma_start(sent_blocks[b, p0:p1, j, :], message[j % 2][p0:p1, :])\
                                    .then_inc(m_stored[j % 2], 16)
                        for p0, p1 in PARTS:
                            sp.dma_start(mid_blocks[b, p0:p1, :, :], res[p0:p1, :, :]).then_inc(stored, 16)
                        sp.wait_ge(stored, 32 * (b + 1))

                    load(h, 0, x_in)
                    sp.wait_ge(cleared, 1)
                    load(res, 0, res_in)
                    with sp.Fori(0, NB - 1) as b:
                        sp.wait_ge(t_done, 2 * (b + 1))
                        load(h, b + 1, x_in)
                        store(b)
                        load(res, b + 1, res_in)
                    sp.wait_ge(t_done, 2 * NB)
                    sp.dma_start(h_wide[:, :, :].rearrange("p k n -> p (k n)"), fused_dram).then_inc(fused_in, 16)
                    store(NB - 1)
                    for signal in m_stored:
                        sp.wait_ge(signal, 32 * (J // 2 * NB + 1))

                @block.gpsimd
                def _(pool):
                    rounds = load_rounds(pool)
                    last_row = pool.to_reg(N - 1)
                    pool.memset(rows.x[:, :], 0.0).then_inc(indexed, 1)
                    pool.memset(res[:, :, :], 0.0).then_inc(cleared, 1)

                    def gather(w):
                        pool.wait_ge(rows.ready, w + 1)
                        pool.wait_ge(more.done, KC * (rounds * w) + 1)
                        pool.wait_ge(indexed, w + 1)
                        pool.sem_inc(gathers, 1)
                        pool.tensor_copy(index[:, :], slot_src[:, bass.ds(w, 1)]).then_inc(indexed, 1)
                        pool.wait_ge(indexed, w + 2)
                        pool.sem_inc(gathers, 1)
                        pool.indirect_dma_start(rows.x[:, :], None, x, bass.IndirectOffsetOnAxis(index[:, :], 0),
                                                bounds_check=last_row, oob_is_err=False).then_inc(rows.gathered, 16)
                        more.on_gpsimd(pool, rounds, w, (g_ready, KC * (w + 1)), last_row)

                    def residual(b):
                        pool.wait_ge(res_in, 32 * (b + 1))
                        pool.tensor_tensor(res[:, :, 0:D], res[:, :, 0:D],
                                           bias[0:P, :].unsqueeze(1).to_broadcast([P, J, D]), ALU.add)
                        pool.tensor_copy(res[:, :, DINV], dinv[:, bass.ds(J * b, J)]).then_inc(biased, 1)

                    gather(0)
                    gather(1)
                    with pool.Fori(0, NB - 1) as b:
                        gather(R * b + 2)
                        residual(b)
                        gather(R * b + 3)
                        gather(R * b + 4)
                    gather(R * NB - 1)
                    residual(NB - 1)

                @block.scalar
                def _(act):
                    rounds = load_rounds(act)

                    def transposed(b, half, free):
                        for c in (2 * half, 2 * half + 1):
                            act.wait_ge(t_done, 2 * b + half + 1)
                            act.wait_ge(agg_added, KC * R * b)
                            act.activation(ht[:, c, :], sum_bank[c % 2][:, 0:BN], ACT.Copy).then_inc(t_copied, 1)
                        if free:
                            act.wait_ge(*free)
                        for c in (2 * half, 2 * half + 1):
                            act.wait_ge(t_copied, KC * b + 2 * half + 2)
                            act.activation(g_hi[1][:, c, :], ht[:, c, :], ACT.Copy).then_inc(self_high, 1)

                    def summed(w, r, half, free):
                        if free:
                            act.wait_ge(*free)
                        for c in (2 * half, 2 * half + 1):
                            act.wait_ge(agg_added, KC * w + c + 1)
                            act.activation(g_hi[r][:, c, :], sum_bank[c % 2][:, 0:BN], ACT.Copy).then_inc(g_high, 1)

                    def hidden(b, s):
                        n = STEPS * b + s
                        z = hid_bank[s % 2][:, 0:BN]
                        act.wait_ge(z_done, n + 1)
                        act.activation(z, z, ACT.Relu, bias=b1_col[:, s:s + 1]).then_inc(z_relued, 1)
                        act.wait_ge(z_relued, n + 1)
                        act.wait_ge(c_done, J * (n + 1))
                        act.activation(hid_hi[s % 2][:, :], z, ACT.Copy).then_inc(z_high, 1)

                    def own(b):
                        for j in range(J):
                            act.activation(h[:, j, :], h[:, j, :], ACT.Relu, bias=nodes.shift[:, j:j + 1],
                                           scale=nodes.y[:, j:j + 1]).then_inc(nodes.ready, 1)

                    def messages(b, half):
                        for j in (2 * half, 2 * half + 1):
                            act.wait_ge(m_stored[j % 2], 32 * (J // 2 * b + j // 2 + 1))
                            act.activation(message[j % 2][:, :], res[:, j, 0:D], ACT.Relu, bias=res[:, j, SHIFT:SHIFT + 1],
                                           scale=res[:, j, SCALE:SCALE + 1]).then_inc(m_made, 1)

                    def body(b, more_blocks):
                        hidden(b, 1)
                        summed(R * b + 1, 1, 0, (self_done, b + 1))
                        hidden(b, 2)
                        summed(R * b + 1, 1, 1, None)
                        more.on_scalar(act, rounds, R * b + 1, sum_bank, g_hi[1])
                        rows.stats_on_scalar(act, R * b + 2)
                        hidden(b, 3)
                        rows.split_on_scalar(act, R * b + 2)
                        hidden(b, 4)
                        summed(R * b + 2, 2, 0, (z_done, STEPS * b + 1))
                        hidden(b, 5)
                        summed(R * b + 2, 2, 1, None)
                        more.on_scalar(act, rounds, R * b + 2, sum_bank, g_hi[2])
                        hidden(b, 6)
                        if more_blocks:
                            nodes.on_scalar(act, b + 1)
                        hidden(b, 7)
                        if more_blocks:
                            own(b + 1)
                            rows.stats_on_scalar(act, R * (b + 1))
                        hidden(b, 8)
                        if more_blocks:
                            rows.split_on_scalar(act, R * (b + 1))
                            transposed(b + 1, 0, (z_done, STEPS * b + 2 * KC))
                        hidden(b, 9)
                        if more_blocks:
                            transposed(b + 1, 1, None)
                        hidden(b, 10)
                        if more_blocks:
                            summed(R * (b + 1), 0, 0, (z_done, STEPS * b + KC))
                        hidden(b, 11)
                        if more_blocks:
                            summed(R * (b + 1), 0, 1, None)
                            more.on_scalar(act, rounds, R * (b + 1), sum_bank, g_hi[0])
                        else:
                            act.wait_ge(fused_in, 16)
                            act.wait_ge(self_done, NB)
                            act.activation(ws_hi[:, :, :], h_wide[:, :, :], ACT.Copy).then_inc(fused_high, 1)
                        outs.on_scalar(act, b)
                        messages(b, 0)
                        if more_blocks:
                            hidden(b + 1, 0)
                            rows.on_scalar(act, R * (b + 1) + 1)
                        messages(b, 1)

                    act.wait_ge(x_in, 32)
                    nodes.on_scalar(act, 0)
                    own(0)
                    rows.on_scalar(act, 0)
                    transposed(0, 0, None)
                    transposed(0, 1, None)
                    summed(0, 0, 0, None)
                    summed(0, 0, 1, None)
                    more.on_scalar(act, rounds, 0, sum_bank, g_hi[0])
                    hidden(0, 0)
                    rows.on_scalar(act, 1)
                    with act.Fori(0, NB - 1) as b:
                        body(b, True)
                    body(NB - 1, False)

                @block.vector
                def _(dve):
                    rounds = load_rounds(dve)

                    def own(b):
                        dve.wait_ge(x_in, 32 * (b + 1))
                        nodes.on_vector(dve, b, h)

                    def transposed(b, half):
                        for c in (2 * half, 2 * half + 1):
                            dve.wait_ge(self_high, KC * b + c + 1)
                            dve.tensor_tensor(g_lo[1][:, c, :], ht[:, c, :], g_hi[1][:, c, :].bitcast(F32), ALU.subtract)\
                                .then_inc(self_ready, 1)

                    def summed(w, r, half):
                        for c in (2 * half, 2 * half + 1):
                            bank = sum_bank[c % 2][:, 0:BN]
                            dve.wait_ge(agg_done, 2 * w + half + 1)
                            dve.tensor_tensor(bank, bank, ht[:, c, :], ALU.add).then_inc(agg_added, 1)
                        for c in (2 * half, 2 * half + 1):
                            dve.wait_ge(g_high, KC * w + c + 1)
                            dve.tensor_tensor(g_lo[r][:, c, :], sum_bank[c % 2][:, 0:BN],
                                              g_hi[r][:, c, :].bitcast(F32), ALU.subtract).then_inc(g_ready, 1)

                    def hidden(b, s):
                        n = STEPS * b + s
                        dve.wait_ge(z_high, n + 1)
                        dve.tensor_tensor(hid_lo[s % 2][:, :], hid_bank[s % 2][:, 0:BN],
                                          hid_hi[s % 2][:, :].bitcast(F32), ALU.subtract).then_inc(hid_ready, 1)

                    def evacuate(b):
                        dve.wait_ge(biased, b + 1)
                        for j in range(J):
                            dve.wait_ge(c_done, J * (STEPS * b + STEPS + 1) + j + 1)
                            dve.tensor_tensor(res[:, j, 0:D], res[:, j, 0:D], out_bank[j][0:P, :], ALU.add)\
                                .then_inc(evacuated, 1)

                    def stats(w):
                        dve.wait_ge(agg_done, 2 * w)
                        rows.stats_on_vector(dve, w, slot_col[:, bass.ds(w, 1)])

                    def body(b, more_blocks):
                        hidden(b, 1)
                        summed(R * b + 1, 1, 0)
                        hidden(b, 2)
                        summed(R * b + 1, 1, 1)
                        more.on_vector(dve, rounds, R * b + 1, sum_bank, g_hi[1], g_lo[1])
                        stats(R * b + 2)
                        hidden(b, 3)
                        rows.split_on_vector(dve, R * b + 2)
                        hidden(b, 4)
                        summed(R * b + 2, 2, 0)
                        hidden(b, 5)
                        summed(R * b + 2, 2, 1)
                        more.on_vector(dve, rounds, R * b + 2, sum_bank, g_hi[2], g_lo[2])
                        hidden(b, 6)
                        if more_blocks:
                            own(b + 1)
                        hidden(b, 7)
                        if more_blocks:
                            stats(R * (b + 1))
                        hidden(b, 8)
                        if more_blocks:
                            rows.split_on_vector(dve, R * (b + 1))
                            transposed(b + 1, 0)
                        hidden(b, 9)
                        if more_blocks:
                            transposed(b + 1, 1)
                        hidden(b, 10)
                        if more_blocks:
                            summed(R * (b + 1), 0, 0)
                        hidden(b, 11)
                        if more_blocks:
                            summed(R * (b + 1), 0, 1)
                            more.on_vector(dve, rounds, R * (b + 1), sum_bank, g_hi[0], g_lo[0])
                        else:
                            dve.wait_ge(fused_high, 1)
                            dve.tensor_tensor(ws_lo[:, :, :], h_wide[:, :, :], ws_hi[:, :, :].bitcast(F32),
                                              ALU.subtract).then_inc(fused_ready, 1)
                        evacuate(b)
                        dve.wait_ge(evacuated, J * (b + 1) + J)
                        outs.on_vector(dve, b, res)
                        if more_blocks:
                            hidden(b + 1, 0)
                            stats(R * (b + 1) + 1)
                            rows.split_on_vector(dve, R * (b + 1) + 1)

                    for ready in (rows.ready, more.done):
                        dve.sem_inc(ready, 1)
                    dve.sem_inc(evacuated, J)
                    dve.sem_inc(hid_ready, 2)
                    own(0)
                    stats(0)
                    rows.split_on_vector(dve, 0)
                    transposed(0, 0)
                    transposed(0, 1)
                    summed(0, 0, 0)
                    summed(0, 0, 1)
                    more.on_vector(dve, rounds, 0, sum_bank, g_hi[0], g_lo[0])
                    hidden(0, 0)
                    stats(1)
                    rows.split_on_vector(dve, 1)
                    with dve.Fori(0, NB - 1) as b:
                        body(b, True)
                    body(NB - 1, False)

                @block.tensor
                def _(pe):
                    rounds = load_rounds(pe)

                    def transpose(b, half):
                        pe.wait_ge(nodes.ready, J * (b + 1))
                        if half:
                            pe.wait_ge(t_copied, KC * b + 2)
                        else:
                            pe.wait_ge(g_ready, KC * R * b)
                        for c in (2 * half, 2 * half + 1):
                            for j in range(J):
                                mm = pe.transpose(sum_bank[c % 2][:, j * P:(j + 1) * P],
                                                  h[:, j, c * 128:(c + 1) * 128], ident[0:P, 0:P])
                        mm.then_inc(t_done, 1)

                    def aggregate(w, half, banks_free):
                        pe.wait_ge(rows.ready, w + 2)
                        pe.wait_ge(*banks_free)
                        for c in (2 * half, 2 * half + 1):
                            mm = pe.matmul(sum_bank[c % 2][:, 0:BN], rows.xr[:, c * 128:(c + 1) * 128],
                                           rows.select[:, :], start=True, stop=True)
                        mm.then_inc(agg_done, 1)

                    def first(b, s):
                        r, m = divmod(s, KC)
                        n = STEPS * b + s
                        if m == 0:
                            pe.wait_ge(g_ready, KC * (R * b + r + 1))
                        pe.wait_ge(hid_ready, n + 1)
                        for k in range(KC):
                            at = r * KC + k
                            mm = split_product(pe, hid_bank[s % 2][:, 0:BN],
                                               (w1_hi[:, at, m * 128:(m + 1) * 128], w1_lo[:, at, m * 128:(m + 1) * 128]),
                                               (g_hi[r][:, k, :], g_lo[r][:, k, :]), k == 0, k == KC - 1)
                        mm.then_inc(z_done, 1)

                    def own(b):
                        pe.wait_ge(self_ready, KC * (b + 1))
                        for j in range(J):
                            pe.wait_ge(evacuated, J * b + j + 1)
                            for k in range(KC):
                                mm = split_product(pe, out_bank[j][0:P, :],
                                                   (g_hi[1][:, k, j * P:(j + 1) * P], g_lo[1][:, k, j * P:(j + 1) * P]),
                                                   (ws_hi[:, k, :], ws_lo[:, k, :]), k == 0, False)
                        mm.then_inc(self_done, 1)

                    def second(b, s):
                        n = STEPS * b + s
                        pe.wait_ge(hid_ready, n + 3)
                        for j in range(J):
                            mm = split_product(pe, out_bank[j][0:P, :],
                                               (hid_hi[s % 2][:, j * P:(j + 1) * P], hid_lo[s % 2][:, j * P:(j + 1) * P]),
                                               (w2_hi[:, s, :], w2_lo[:, s, :]), False, s == STEPS - 1)
                            if s == STEPS - 1:
                                mm.then_inc(c_done, 1)
                        if s < STEPS - 1:
                            mm.then_inc(c_done, J)

                    def body(b, more_blocks):
                        w = R * b
                        first(b, 0)
                        own(b)
                        first(b, 1)
                        second(b, 0)
                        aggregate(w + 1, 0, (g_ready, KC * (w + 1)))
                        first(b, 2)
                        second(b, 1)
                        aggregate(w + 1, 1, (g_ready, KC * (w + 1) + 2))
                        more.on_tensor(pe, rounds, w + 1, sum_bank)
                        first(b, 3)
                        second(b, 2)
                        first(b, 4)
                        second(b, 3)
                        aggregate(w + 2, 0, (g_ready, KC * (w + 2)))
                        first(b, 5)
                        second(b, 4)
                        aggregate(w + 2, 1, (g_ready, KC * (w + 2) + 2))
                        more.on_tensor(pe, rounds, w + 2, sum_bank)
                        for s in (6, 7, 8):
                            first(b, s)
                            second(b, s - 1)
                        if more_blocks:
                            transpose(b + 1, 0)
                        first(b, 9)
                        second(b, 8)
                        if more_blocks:
                            transpose(b + 1, 1)
                        first(b, 10)
                        second(b, 9)
                        if more_blocks:
                            aggregate(w + 3, 0, (t_copied, KC * (b + 2)))
                        first(b, 11)
                        second(b, 10)
                        if more_blocks:
                            aggregate(w + 3, 1, (g_ready, KC * (w + 3) + 2))
                            more.on_tensor(pe, rounds, w + 3, sum_bank)
                        second(b, 11)

                    for free in m_stored:
                        pe.sem_inc(free, 32)
                    pe.sem_inc(c_done, 2 * J)
                    transpose(0, 0)
                    transpose(0, 1)
                    aggregate(0, 0, (t_copied, KC))
                    aggregate(0, 1, (g_ready, 2))
                    more.on_tensor(pe, rounds, 0, sum_bank)
                    with pe.Fori(0, NB - 1) as b:
                        body(b, True)
                    body(NB - 1, False)

        layer1 = ExitStack()
        with layer1:
            RES, TURN, TILES = 4, 4, 2 * R
            h = sb("h1", [P, J, D], F32, layer1)
            res = [sb(f"res1_{i}", [P, J, XW], F32, layer1) for i in range(RES)]
            ht = sb("ht1", [128, KC, BN], F32, layer1)
            g_hi = [sb(f"u_hi{i}", [128, KC, BN], F32R, layer1) for i in range(2)]
            g_lo = [sb(f"u_lo{i}", [128, KC, BN], F32R, layer1) for i in range(2)]
            index = [sb(f"index1_{i}", [128, 1], I32, layer1) for i in range(TILES)]
            rows = [Rows(f"rows1_{i}", layer1, False) for i in range(TILES)]
            more = Rounds("more1", layer1, sent, Rows("more_rows1", layer1, False))
            out_bank = [layer1.enter_context(nc.psum_tensor(f"y_bank{j}", [128, 512], F32)) for j in range(J)]
            sum_bank = [layer1.enter_context(nc.psum_tensor(f"u_bank{c}", [128, 512], F32)) for c in range(KC)]

            bias_in, cleared = sem("bias_in1"), sem("cleared1")
            res_in = [sem(f"mid_in{i}") for i in range(RES)]
            stored = [sem(f"out_stored{i}") for i in range(RES)]
            indexed, gathers = sem("indexed1"), sem("gathers1")
            rows_used = sem("rows_used1")
            h_ready, t_done, t_copied = sem("h_ready1"), sem("t_done1"), sem("t_copied1")
            agg_added, g_high, g_ready = sem("agg_added1"), sem("g_high1"), sem("g_ready1")
            out_done, evacuated, biased = sem("out_done1"), sem("evacuated1"), sem("biased1")

            def tile_of(r, turn, place):
                return rows[R * (place % 2) + r], TURN // 2 * turn + place // 2

            def turns(engine, body):
                with engine.Fori(0, NB // TURN - 1) as t:
                    for i in range(TURN):
                        body(TURN * t + i, t, i, NB)
                for i in range(TURN):
                    body(NB - TURN + i, NB // TURN - 1, i, TURN - i)

            with nc.Block() as block:
                @block.sync
                def _(sp):
                    def load(b, slot):
                        for p0, p1 in PARTS:
                            sp.dma_start(res[slot][p0:p1, :, :], mid_blocks[b, p0:p1, :, :]).then_inc(res_in[slot], 16)

                    def body(b, turn, i, left):
                        sp.wait_ge(evacuated, J * (b + 1) + J)
                        for p0, p1 in PARTS:
                            sp.dma_start(out_blocks[b, p0:p1, :, :], res[i][p0:p1, :, 0:D]).then_inc(stored[i], 16)
                        sp.wait_ge(stored[i], 32 * (turn + 1))
                        if left > RES:
                            load(b + RES, i)

                    load(0, 0)
                    sp.dma_start(bias[:, :], bias2_dram).then_inc(bias_in, 16)
                    for i in range(1, RES):
                        load(i, i)
                    turns(sp, body)

                @block.gpsimd
                def _(pool):
                    rounds = load_rounds(pool)
                    last_row = pool.to_reg(N - 1)

                    def gather(b, place):
                        for r in range(R):
                            w, tile = R * b + r, R * (place % 2) + r
                            pool.wait_ge(rows_used, w + 1)
                            pool.tensor_copy(index[tile][:, :], slot_src[:, bass.ds(w, 1)]).then_inc(indexed, 1)
                            pool.wait_ge(indexed, w + 1)
                            pool.sem_inc(gathers, 1)
                            pool.indirect_dma_start(rows[tile].x[:, :], None, sent,
                                                    bass.IndirectOffsetOnAxis(index[tile][:, :], 0),
                                                    bounds_check=last_row, oob_is_err=False)\
                                .then_inc(rows[tile].gathered, 16)

                    def add_bias(b, place):
                        pool.wait_ge(h_ready, J * (b + 1))
                        to = res[place % RES]
                        pool.tensor_tensor(to[:, :, 0:D], to[:, :, 0:D],
                                           bias[0:P, :].unsqueeze(1).to_broadcast([P, J, D]), ALU.add)\
                            .then_inc(biased, 1)

                    def body(b, turn, i, left):
                        if left > 2:
                            gather(b + 2, i + 2)
                        if left > 1:
                            add_bias(b + 1, i + 1)
                            for r in range(R):
                                more.on_gpsimd(pool, rounds, R * (b + 1) + r, (g_ready, KC * (b + 2)), last_row)

                    for tile in range(TILES):
                        pool.memset(rows[tile].x[:, :], 0.0)
                    clear = pool.memset(more.rows.x[:, :], 0.0)
                    clear.then_inc(cleared, 1)
                    pool.wait_ge(cleared, 1)
                    gather(0, 0)
                    gather(1, 1)
                    pool.wait_ge(bias_in, 16)
                    add_bias(0, 0)
                    for r in range(R):
                        more.on_gpsimd(pool, rounds, r, (g_ready, KC), last_row)
                    turns(pool, body)

                @block.scalar
                def _(act):
                    rounds = load_rounds(act)

                    def own(b, turn, place):
                        slot = place % RES
                        act.wait_ge(res_in[slot], 32 * (turn + place // RES + 1))
                        for j in range(J):
                            act.activation(h[:, j, :], res[slot][:, j, 0:D], ACT.Relu,
                                           bias=res[slot][:, j, SHIFT:SHIFT + 1],
                                           scale=res[slot][:, j, SCALE:SCALE + 1]).then_inc(h_ready, 1)

                    def split(turn, place):
                        for r in range(R):
                            tile, n = tile_of(r, turn, place)
                            tile.on_scalar(act, n)

                    def transposed(b):
                        for c in range(KC):
                            act.wait_ge(t_done, KC * b + c + 1)
                            act.activation(ht[:, c, :], sum_bank[c][:, 0:BN], ACT.Copy).then_inc(t_copied, 1)

                    def summed(b, place):
                        for c in range(KC):
                            act.wait_ge(agg_added, KC * b + c + 1)
                            act.activation(g_hi[place % 2][:, c, :], sum_bank[c][:, 0:BN], ACT.Copy).then_inc(g_high, 1)
                        for r in range(R):
                            more.on_scalar(act, rounds, R * b + r, sum_bank, g_hi[place % 2])

                    def body(b, turn, i, left):
                        if left > 1:
                            act.wait_ge(out_done, J * b + 1)
                            summed(b + 1, i + 1)
                        if left > 2:
                            split(turn, i + 2)
                            transposed(b + 2)
                        if left > 3:
                            own(b + 3, turn, i + 3)

                    own(0, 0, 0)
                    transposed(0)
                    split(0, 0)
                    own(1, 0, 1)
                    split(0, 1)
                    summed(0, 0)
                    transposed(1)
                    own(2, 0, 2)
                    turns(act, body)

                @block.vector
                def _(dve):
                    rounds = load_rounds(dve)

                    def split(b, turn, place):
                        for r in range(R):
                            tile, n = tile_of(r, turn, place)
                            dve.wait_ge(rows_used, R * b + r + 1)
                            tile.on_vector(dve, n, slot_col[:, bass.ds(R * b + r, 1)])

                    def summed(b, place):
                        hi, lo = g_hi[place % 2], g_lo[place % 2]
                        dve.wait_ge(rows_used, R * (b + 1) + TILES)
                        for c in range(KC):
                            bank = sum_bank[c][:, 0:BN]
                            dve.tensor_tensor(bank, bank, ht[:, c, :], ALU.add).then_inc(agg_added, 1)
                        for c in range(KC):
                            dve.wait_ge(g_high, KC * b + c + 1)
                            dve.tensor_tensor(lo[:, c, :], sum_bank[c][:, 0:BN], hi[:, c, :].bitcast(F32),
                                              ALU.subtract).then_inc(g_ready, 1)
                        for r in range(R):
                            more.on_vector(dve, rounds, R * b + r, sum_bank, hi, lo)

                    def evacuate(b, i):
                        dve.wait_ge(biased, b + 1)
                        for j in range(J):
                            dve.wait_ge(out_done, J * b + j + 2)
                            dve.scalar_tensor_tensor(res[i][:, j, 0:D], out_bank[j][0:P, :], res[i][:, j, DINV:DINV + 1],
                                                     res[i][:, j, 0:D], ALU.mult, ALU.add).then_inc(evacuated, 1)

                    def body(b, turn, i, left):
                        if left > 1:
                            summed(b + 1, i + 1)
                        if left > 2:
                            split(b + 2, turn, i + 2)
                        evacuate(b, i)

                    dve.sem_inc(evacuated, J)
                    dve.sem_inc(more.done, 1)
                    split(0, 0, 0)
                    summed(0, 0)
                    split(1, 0, 1)
                    turns(dve, body)

                @block.tensor
                def _(pe):
                    rounds = load_rounds(pe)

                    def transpose(b):
                        pe.wait_ge(h_ready, J * (b + 1))
                        for c in range(KC):
                            for j in range(J):
                                mm = pe.transpose(sum_bank[c][:, j * P:(j + 1) * P],
                                                  h[:, j, c * 128:(c + 1) * 128], ident[0:P, 0:P])
                            mm.then_inc(t_done, 1)

                    def aggregate(b, turn, place):
                        for r in range(R):
                            tile, n = tile_of(r, turn, place)
                            pe.wait_ge(tile.ready, n + 1)
                            for c in range(KC):
                                if r == 0:
                                    pe.wait_ge(t_copied, KC * b + c + 1)
                                mm = pe.matmul(sum_bank[c][:, 0:BN], tile.xr[:, c * 128:(c + 1) * 128],
                                               tile.select[:, :], start=(r == 0), stop=(r == R - 1))
                            mm.then_inc(rows_used, 1)
                        for r in range(R):
                            more.on_tensor(pe, rounds, R * b + r, sum_bank)

                    def multiply(b, i, j):
                        pe.wait_ge(evacuated, J * b + j + 1)
                        for k in range(KC):
                            mm = split_product(pe, out_bank[j][0:P, :],
                                               (g_hi[i % 2][:, k, j * P:(j + 1) * P],
                                                g_lo[i % 2][:, k, j * P:(j + 1) * P]),
                                               (ws_hi[:, k, :], ws_lo[:, k, :]), k == 0, k == KC - 1)
                        mm.then_inc(out_done, 1)

                    def body(b, turn, i, left):
                        if left > 1:
                            aggregate(b + 1, turn, i + 1)
                        pe.wait_ge(g_ready, KC * (b + 1))
                        for j in range(J - 1):
                            multiply(b, i, j)
                        if left > 2:
                            pe.wait_ge(g_ready, KC * (b + 2))
                            transpose(b + 2)
                        multiply(b, i, J - 1)

                    pe.sem_inc(rows_used, TILES)
                    pe.sem_inc(out_done, 1)
                    transpose(0)
                    aggregate(0, 0, 0)
                    pe.wait_ge(g_ready, KC)
                    transpose(1)
                    turns(pe, body)


_INS = ['x', 'src', 'dst', 'edge_type_3', 'L0_gnn_W_self', 'L0_gnn_b_self', 'L0_gnn_W1', 'L0_gnn_b1',
        'L0_gnn_W2', 'L0_gnn_b2', 'L1_gnn_W_gcn', 'L1_gnn_b_gcn', 'L1_gnn_W_dense', 'L1_gnn_b_dense']


def kernel(**inputs):
    import numpy as np
    import concourse.bacc as bacc
    from concourse.bass_utils import run_bass_kernel_spmd

    nc = bacc.Bacc("TRN2", target_bir_lowering=False, num_devices=1)
    arrays = {f"in_{name}": np.ascontiguousarray(inputs[name]) for name in _INS}
    args = [nc.dram_tensor(name, a.shape, mybir.dt.from_np(a.dtype), kind="ExternalInput").ap()
            for name, a in arrays.items()]
    out = nc.dram_tensor("out", arrays["in_x"].shape, mybir.dt.float32, kind="ExternalOutput").ap()
    build_program(nc, *args, out)
    return run_bass_kernel_spmd(nc, [arrays], core_ids=[0]).results[0]["out"]
```

```python
from contextlib import ExitStack

import concourse.bass as bass
from concourse import mybir


def build_program(nc, x, src, dst, edge_type, w_self, b_self, w1, b1, w2, b2, w_gcn, b_gcn, w_dense, b_dense, out):
    F32, F32R, BF16, I32 = mybir.dt.float32, mybir.dt.float32r, mybir.dt.bfloat16, mybir.dt.int32
    ALU, ACT, AX = mybir.AluOpType, mybir.ActivationFunctionType, mybir.AxisListType

    N, D = x.shape
    E = src.shape[0]
    R = w1.shape[0]
    P, J = 125, 4
    BN = P * J
    NB = N // BN
    KC = D // 128
    W = NB * R
    EJ = E // P
    SLOTS = 64
    MAXR = -(-E // SLOTS)
    XW = D + 4
    DINV, SCALE, SHIFT = D, D + 1, D + 2
    EPS = 1e-5
    ROUND = 12582912.0
    ABSENT = 2.0 * N
    STEPS = R * KC
    assert NB * BN == N and KC * 128 == D and EJ * P == E
    PARTS = ((0, 112), (112, P))

    x_blocks = x.rearrange("(b p j) d -> b p j d", p=P, j=J)
    out_blocks = out.rearrange("(b p j) d -> b p j d", p=P, j=J)
    mid = nc.dram_tensor("mid", [N, XW], F32, kind="Internal").ap()
    mid_blocks = mid.rearrange("(b p j) d -> b p j d", p=P, j=J)
    fused_dram = nc.dram_tensor("fused_w", [128, KC * D], F32, kind="Internal").ap()
    bias2_dram = nc.dram_tensor("bias2", [128, D], F32, kind="Internal").ap()
    slots_dram = nc.dram_tensor("slots", [MAXR, 128, 2, W], I32, kind="Internal").ap()

    class Chain:

        def __init__(self, engine, sem, at=0):
            self.engine, self.sem, self.at, self.n = engine, sem, at, 0

        def link(self, instruction):
            self.n += 1
            instruction.then_inc(self.sem, 1)
            self.engine.wait_ge(self.sem, self.at + self.n)

    with ExitStack() as ctx:
        def sb(name, shape, dt=F32, into=ctx):
            return into.enter_context(nc.sbuf_tensor(name, shape, dt))

        def sem(name):
            return ctx.enter_context(nc.semaphore(name))

        def low_in_place(name, shape, into=ctx):
            with ExitStack() as at:
                whole = sb(name + "_whole", shape, F32, at)
            return whole, sb(name + "_lo", shape, F32R, into)

        ws_hi, (ws_whole, ws_lo) = sb("ws_hi", [128, KC, D], F32R), low_in_place("ws", [128, KC, D])
        bias = sb("bias", [128, D])
        b1_col = sb("b1_col", [128, STEPS])
        ident = sb("ident", [128, 128])
        node_iota = sb("node_iota", [128, BN])
        dinv = sb("dinv", [P, NB * J])
        slots = sb("slots_sb", [128, 2, W], I32)
        slot_src, slot_col = slots[:, 0, :], slots[:, 1, :].bitcast(F32)
        rounds_sb = sb("rounds_sb", [128, 1], I32)

        layer0 = ExitStack()
        w1_hi, w2_hi = (sb(n, [128, R * KC, D], F32R, layer0) for n in ("w1_hi", "w2_hi"))
        (w1_whole, w1_lo), (w2_whole, w2_lo) = (low_in_place(n, [128, R * KC, D], layer0) for n in ("w1", "w2"))
        h_wide = sb("h0", [128, J, D], F32, layer0)
        h = h_wide[0:P]
        x_in = sem("x_in")

        class Rows:
            LINKS = 6

            def __init__(self, name, into, norm, share=None):
                self.norm = norm
                if share:
                    self.x, self.y, self.xr, self.select, self.small = share.x, share.y, share.xr, share.select, share.small
                else:
                    self.x = sb(name + "_x", [128, D if norm else XW], F32, into)
                    self.y = self.x if norm else sb(name + "_y", [128, D], F32, into)
                    self.xr = sb(name + "_xr", [128, D], F32R, into)
                    self.select = sb(name + "_select", [128, BN], F32R, into)
                    self.small = sb(name + "_small", [128, 16], F32, into) if norm else None
                self.gathered, self.relued = sem(name + "_gathered"), sem(name + "_relued")
                if norm:
                    self.chain, self.norm_ready = sem(name + "_chain"), sem(name + "_norm_ready")
                    self.var_ready, self.root_ready = sem(name + "_var_ready"), sem(name + "_root_ready")
                self.high_ready, self.ready = sem(name + "_high_ready"), sem(name + "_ready")

            def stats_on_vector(self, dve, n, column):
                if not self.norm:
                    dve.tensor_scalar(self.select[:, :], node_iota[:, :], column, None, ALU.is_equal)
                    return
                link = Chain(dve, self.chain, self.LINKS * n).link
                stat, mean, var = self.small[:, 0:6], self.small[:, 6:7], self.small[:, 7:8]
                v, root, y, t, shift = (self.small[:, i:i + 1] for i in range(8, 13))
                dve.wait_ge(self.gathered, 16 * (n + 1))
                link(dve.bn_stats(stat, self.x[:, :]))
                dve.tensor_scalar(self.select[:, :], node_iota[:, :], column, None, ALU.is_equal)
                link(dve.bn_aggr(self.small[:, 6:8], stat))
                dve.tensor_scalar(v, var, EPS, None, ALU.add).then_inc(self.var_ready, 1)
                dve.wait_ge(self.root_ready, n + 1)
                link(dve.reciprocal(y, root))
                link(dve.scalar_tensor_tensor(t, y, y, v, ALU.mult, ALU.mult))
                link(dve.tensor_scalar(t, t, -0.5, 1.5, ALU.mult, ALU.add))
                link(dve.tensor_tensor(y, y, t, ALU.mult))
                dve.scalar_tensor_tensor(shift, mean, -1.0, y, ALU.mult, ALU.mult).then_inc(self.norm_ready, 1)

            def split_on_vector(self, dve, n):
                dve.wait_ge(self.high_ready, n + 1)
                dve.tensor_tensor(self.xr[SLOTS:128, :], self.y[SLOTS:128, :], self.xr[SLOTS:128, :].bitcast(F32),
                                  ALU.subtract).then_inc(self.ready, 1)

            def stats_on_scalar(self, act, n):
                if self.norm:
                    act.wait_ge(self.var_ready, n + 1)
                    act.activation(self.small[:, 9:10], self.small[:, 8:9], ACT.Sqrt).then_inc(self.root_ready, 1)

            def split_on_scalar(self, act, n):
                if self.norm:
                    act.wait_ge(self.norm_ready, n + 1)
                    shift, scale = self.small[:, 12:13], self.small[:, 10:11]
                else:
                    act.wait_ge(self.gathered, 16 * (n + 1))
                    shift, scale = self.x[:, SHIFT:SHIFT + 1], self.x[:, SCALE:SCALE + 1]
                act.activation(self.y[:, :], self.x[:, 0:D], ACT.Relu, bias=shift, scale=scale).then_inc(self.relued, 1)
                act.wait_ge(self.relued, n + 1)
                act.activation(self.xr[:, :], self.y[:, :], ACT.Copy).then_inc(self.high_ready, 1)

            def on_vector(self, dve, n, column):
                self.stats_on_vector(dve, n, column)
                self.split_on_vector(dve, n)

            def on_scalar(self, act, n):
                self.stats_on_scalar(act, n)
                self.split_on_scalar(act, n)

        class Nodes:
            LINKS = 7

            def __init__(self, name, into, degree):
                self.degree = degree
                self.stat = sb(name + "_stat", [P, J, 6], F32, into)
                self.mean_var = sb(name + "_mean_var", [P, J, 2], F32, into)
                self.v, self.root, self.y, self.t, self.shift = (
                    sb(name + n, [P, J], F32, into) for n in ("_v", "_root", "_y", "_t", "_shift"))
                self.chain, self.var_ready, self.root_ready = (
                    sem(name + "_chain"), sem(name + "_var_ready"), sem(name + "_root_ready"))
                self.norm_ready, self.ready = sem(name + "_norm_ready"), sem(name + "_ready")

            def on_vector(self, dve, b, source):
                link = Chain(dve, self.chain, (self.LINKS + self.degree) * b).link
                for j in range(J):
                    step = dve.bn_stats(self.stat[:, j, :], source[:, j, 0:D])
                link(step)
                dve.memset(self.t[:, :], 0.0)
                for j in range(J):
                    step = dve.bn_aggr(self.mean_var[:, j, :], self.stat[:, j, :])
                link(step)
                dve.tensor_scalar(self.v[:, :], self.mean_var[:, :, 1], EPS, None, ALU.add)\
                    .then_inc(self.var_ready, 1)
                dve.wait_ge(self.root_ready, b + 1)
                y, t = self.y[:, :], self.t[:, :]
                link(dve.reciprocal(y, self.root[:, :]))
                link(dve.tensor_tensor(t, y, y, ALU.mult))
                link(dve.tensor_tensor(t, t, self.v[:, :], ALU.mult))
                link(dve.tensor_scalar(t, t, -0.5, 1.5, ALU.mult, ALU.add))
                link(dve.tensor_tensor(y, y, t, ALU.mult))
                scale, shift = y, self.shift[:, :]
                if self.degree:
                    scale, shift = source[:, :, SCALE], source[:, :, SHIFT]
                    link(dve.tensor_tensor(scale, y, source[:, :, DINV], ALU.mult))
                dve.scalar_tensor_tensor(shift, self.mean_var[:, :, 0], -1.0, scale, ALU.mult, ALU.mult)\
                    .then_inc(self.norm_ready, 1)

            def root_on_scalar(self, act, b):
                act.wait_ge(self.var_ready, b + 1)
                act.activation(self.root[:, :], self.v[:, :], ACT.Sqrt).then_inc(self.root_ready, 1)

            def relu_on_scalar(self, act, b, rows):
                act.wait_ge(self.norm_ready, b + 1)
                for j in range(J):
                    act.activation(rows[:, j, :], rows[:, j, :], ACT.Relu, bias=self.shift[:, j:j + 1],
                                   scale=self.y[:, j:j + 1]).then_inc(self.ready, 1)

        def split_product(pe, bank, stationary, moving, start, stop):
            (s_hi, s_lo), (m_hi, m_lo) = stationary, moving
            pe.matmul(bank, s_hi, m_hi, start=start, stop=False)
            pe.matmul(bank, s_hi, m_lo, start=False, stop=False)
            return pe.matmul(bank, s_lo, m_hi, start=False, stop=stop)

        class Rounds:

            def __init__(self, name, into, source, rows):
                self.source, self.rows = source, rows
                self.entry = sb(name + "_entry", [128, 2], I32, into)
                self.index, self.column = self.entry[:, 0:1], self.entry[:, 1:2].bitcast(F32)
                self.table, self.gathers, self.chain = sem(name + "_table"), sem(name + "_gathers"), sem(name + "_chain")
                self.summed, self.added = sem(name + "_summed"), sem(name + "_added")
                self.high, self.done = sem(name + "_high"), sem(name + "_done")

            def each(self, engine, rounds, w, body):
                with engine.If(rounds > 0):
                    with engine.Fori(0, rounds) as k:
                        body(w * rounds + k, k)

            def on_gpsimd(self, pool, rounds, w, first_done, last_row):
                def body(n, k):
                    pool.wait_ge(*first_done)
                    pool.wait_ge(self.done, KC * n + 1)
                    with nc.allow_non_contiguous_dma(reason="one value to a partition"):
                        pool.dma_start(self.entry[:, :].unsqueeze(2), slots_dram[k, :, :, bass.ds(w, 1)])\
                            .then_inc(self.table, 16)
                    pool.wait_ge(self.table, 16 * (n + 1))
                    pool.sem_inc(self.gathers, 1)
                    pool.indirect_dma_start(self.rows.x[:, :], None, self.source,
                                            bass.IndirectOffsetOnAxis(self.index, 0),
                                            bounds_check=last_row, oob_is_err=False).then_inc(self.rows.gathered, 16)
                self.each(pool, rounds, w, body)

            def on_vector(self, dve, rounds, w, banks, hi, lo):
                def body(n, k):
                    dve.wait_ge(self.rows.gathered, 16 * (n + 1))
                    self.rows.on_vector(dve, n, self.column)
                    for c in range(KC):
                        bank = banks[c % len(banks)][:, 0:BN]
                        dve.wait_ge(self.summed, KC * n + c + 1)
                        Chain(dve, self.chain, KC * n + c).link(
                            dve.tensor_tensor(bank, bank, lo[:, c, :].bitcast(F32), ALU.add))
                        dve.tensor_tensor(bank, bank, hi[:, c, :].bitcast(F32), ALU.add).then_inc(self.added, 1)
                        dve.wait_ge(self.high, KC * n + c + 1)
                        dve.tensor_tensor(lo[:, c, :], bank, hi[:, c, :].bitcast(F32), ALU.subtract)\
                            .then_inc(self.done, 1)
                self.each(dve, rounds, w, body)

            def on_scalar(self, act, rounds, w, banks, hi):
                def body(n, k):
                    self.rows.on_scalar(act, n)
                    for c in range(KC):
                        act.wait_ge(self.added, KC * n + c + 1)
                        act.activation(hi[:, c, :], banks[c % len(banks)][:, 0:BN], ACT.Copy).then_inc(self.high, 1)
                self.each(act, rounds, w, body)

            def on_tensor(self, pe, rounds, w, banks):
                def body(n, k):
                    pe.wait_ge(self.rows.ready, n + 1)
                    for c in range(KC):
                        if c >= len(banks):
                            pe.wait_ge(self.done, KC * n + c + 1 - len(banks) + 1)
                        pe.matmul(banks[c % len(banks)][:, 0:BN], self.rows.xr[:, c * 128:(c + 1) * 128],
                                  self.rows.select[:, :], start=True, stop=True).then_inc(self.summed, 1)
                    pe.wait_ge(self.done, KC * (n + 1) + 1)
                self.each(pe, rounds, w, body)

        def load_rounds(engine):
            return engine.value_load(rounds_sb[0:1, 0:1], min_val=0, max_val=MAXR - 1)

        nodes = Nodes("nodes0", layer0, 0)
        prep = ExitStack()
        with prep:
            def tmp(name, shape, dt=F32):
                return sb(name, shape, dt, prep)

            gcn, gcn_t, dense = tmp("gcn", [128, KC, D]), tmp("gcn_t", [128, KC, D]), tmp("dense", [128, KC, D])
            ints = tmp("ints", [P, 3, EJ], I32)
            srcf, dstf, typef = (tmp(n, [P, EJ]) for n in ("srcf", "dstf", "typef"))
            blk, loc, prt, row4, col, bucket, qidx, rank = (
                tmp(n, [P, EJ]) for n in ("blk", "loc", "prt", "row4", "col", "bucket", "qidx", "rank"))
            hot = tmp("hot", [P, EJ, W])
            before = tmp("before", [P, EJ, W])
            pairs = tmp("pairs", [P, EJ, 2, W])
            pick = tmp("pick", [P, EJ, 128])
            hot_p, hot_q = tmp("hot_p", [P, EJ, P], BF16), tmp("hot_q", [P, EJ, NB * J], BF16)
            row_sum = tmp("row_sum", [P, W])
            iota_w, iota_p, iota_q, iota_s = (
                tmp(n, [P, k]) for n, k in (("iota_w", W), ("iota_p", P), ("iota_q", NB * J), ("iota_s", 128)))
            tri = tmp("tri", [P, P])
            ones = tmp("ones", [P, 128])
            b1_rows, bg_rows = tmp("b1_rows", [STEPS, 128]), tmp("bg_rows", [KC, 128])
            bg_col = tmp("bg_col", [128, KC])
            bias_rows, dense_row = tmp("bias_rows", [R + 1, D]), tmp("dense_row", [1, D])
            bias2 = tmp("bias2_sb", [128, D])
            deg, root, y2 = tmp("deg", [P, NB * J]), tmp("root", [P, NB * J]), tmp("y2", [P, NB * J])
            top = tmp("top", [128, 2])
            empty = tmp("empty", [128, W])
            psum = ExitStack()
            with psum:
                def pb(name, shape):
                    return psum.enter_context(nc.psum_tensor(name, shape, F32))

                p_rank, p_count, p_slots, p_deg, p_cols = (
                    pb(n, [128, 512]) for n in ("p_rank", "p_count", "p_slots", "p_deg", "p_cols"))
                p_fuse = [pb(f"p_fuse{i}", [128, 512]) for i in range(3)]

                weights = [(w_self, ws_whole[:, :, :], ws_hi[:, :, :], ws_lo[:, :, :])]
                for w, whole, hi, lo in ((w1, w1_whole, w1_hi, w1_lo), (w2, w2_whole, w2_hi, w2_lo)):
                    for r in range(R):
                        at = slice(r * KC, (r + 1) * KC)
                        weights.append((w[r], whole[:, at, :], hi[:, at, :], lo[:, at, :]))
                ON_POOL = range(0, 5)

                edges_in, consts = sem("edges_in"), sem("consts")
                w_in, w_high = [sem(f"w_in{i}") for i in range(len(weights))], sem("w_high")
                gcn_in, dense_in, bias_in = sem("gcn_in"), sem("dense_in"), sem("bias_in")
                chain_p, chain_g = sem("chain_p"), sem("chain_g")
                sums_ready, ranks_up, picked, slots_up = (
                    sem("sums_ready"), sem("ranks_up"), sem("picked"), sem("slots_up"))
                slots_out, slots_stored, tables_free = sem("slots_out"), sem("slots_stored"), sem("tables_free")
                hots_ready, deg_up, deg_ready, root_ready = (
                    sem("hots_ready"), sem("deg_up"), sem("deg_ready"), sem("root_ready"))
                rounds_ready = sem("rounds_ready")
                cols_up, cols_copied = sem("cols_up"), sem("cols_copied")
                gt_up, gt_copied, fused_up, fused_copied, fused_out = (
                    sem("gt_up"), sem("gt_copied"), sem("fused_up"), sem("fused_copied"), sem("fused_out"))
                bias_up, bias2_up, bias2_copied = sem("bias_up"), sem("bias2_up"), sem("bias2_copied")

                def low_part(engine, i):
                    _, whole, hi, lo = weights[i]
                    engine.wait_ge(w_high, i + 1)
                    engine.tensor_tensor(lo, whole, hi.bitcast(F32), ALU.subtract)

                with nc.Block() as block:
                    @block.sync
                    def _(sp):
                        for i, a in enumerate((dst, edge_type, src)):
                            sp.dma_start(ints[:, i, :], a.rearrange("(p i) -> p i", p=P)).then_inc(edges_in, 16)
                        sp.dma_start(gcn[:, :, :], w_gcn.rearrange("(k p) n -> p k n", p=128)).then_inc(gcn_in, 16)
                        sp.dma_start(dense[:, :, :], w_dense.rearrange("(k p) n -> p k n", p=128))\
                            .then_inc(dense_in, 16)
                        for i, (w, whole, _, _) in enumerate(weights):
                            if i == 3:
                                for p0, p1 in PARTS:
                                    sp.dma_start(h[p0:p1, :, :], x_blocks[0, p0:p1, :, :]).then_inc(x_in, 16)
                            sp.dma_start(whole, w.rearrange("(k p) n -> p k n", p=128)).then_inc(w_in[i], 16)
                        sp.wait_ge(fused_copied, KC)
                        sp.dma_start(fused_dram, gcn[:, :, :].rearrange("p k n -> p (k n)")).then_inc(fused_out, 16)
                        sp.wait_ge(bias2_copied, 1)
                        sp.dma_start(bias2_dram, bias2[:, :]).then_inc(fused_out, 16)
                        sp.wait_ge(fused_out, 32)

                    @block.gpsimd
                    def _(pool):
                        link = Chain(pool, chain_g).link
                        pool.iota(iota_w[:, :], [[1, W]], base=0, channel_multiplier=0,
                                  allow_small_or_imprecise_dtypes=True)
                        pool.memset(ones[:, :], 1.0)
                        pool.memset(tri[:, :], 1.0)
                        link(pool.memset(ident[:, :], 0.0))
                        link(pool.affine_select(out=ident[:, :], in_=ident[:, :], compare_op=ALU.not_equal, fill=1.0,
                                                base=0, pattern=[[-1, 128]], channel_multiplier=1))
                        pool.affine_select(out=tri[:, :], in_=tri[:, :], compare_op=ALU.is_ge, fill=0.0,
                                           base=-1, pattern=[[1, P]], channel_multiplier=-1).then_inc(consts, 1)
                        for t, k in ((iota_p, P), (iota_q, NB * J)):
                            pool.iota(t[:, :], [[1, k]], base=0, channel_multiplier=0,
                                      allow_small_or_imprecise_dtypes=True)
                        pool.iota(node_iota[:, :], [[1, BN]], base=0, channel_multiplier=0,
                                  allow_small_or_imprecise_dtypes=True)
                        pool.iota(iota_s[:, :].rearrange("p (a s) -> p a s", a=2), [[0, 2], [1, SLOTS]], base=0,
                                  channel_multiplier=0, allow_small_or_imprecise_dtypes=True).then_inc(consts, 1)
                        for i in ON_POOL:
                            low_part(pool, i)
                        pool.wait_ge(rounds_ready, 1)
                        rounds = pool.value_load(rounds_sb[0:1, 0:1], min_val=0, max_val=MAXR - 1)
                        with pool.If(rounds > 0):
                            with pool.Fori(0, rounds) as k:
                                pool.wait_ge(slots_out, 4 * (k + 1))
                                pool.dma_start(slots_dram[k], slots[:, :, :]).then_inc(slots_stored, 16)
                                pool.wait_ge(slots_stored, 16 * (k + 1))
                                pool.sem_inc(tables_free, 1)

                    @block.scalar
                    def _(act):
                        act.dma_start(b1_rows[:, :], b1.rearrange("r (m p) -> (r m) p", p=128)).then_inc(bias_in, 16)
                        act.dma_start(bg_rows[:, :], b_gcn.rearrange("(m p) -> m p", p=128)).then_inc(bias_in, 16)
                        act.dma_start(bias_rows[0:1, :], b_self[None, :]).then_inc(bias_in, 16)
                        act.dma_start(bias_rows[1:R + 1, :], b2).then_inc(bias_in, 16)
                        act.dma_start(dense_row[:, :], b_dense[None, :]).then_inc(bias_in, 16)

                        def high(i):
                            _, whole, hi, _ = weights[i]
                            act.wait_ge(w_in[i], 16)
                            act.activation(hi, whole, ACT.Copy).then_inc(w_high, 1)

                        def fused(m):
                            act.wait_ge(fused_up, m + 1)
                            act.activation(gcn[:, m, :], p_fuse[m % 2][:, :], ACT.Copy).then_inc(fused_copied, 1)

                        for k in range(KC):
                            act.wait_ge(gt_up, k + 1)
                            act.activation(gcn_t[:, k, :], p_fuse[k % 2][:, :], ACT.Copy).then_inc(gt_copied, 1)
                        high(0)
                        fused(0)
                        fused(1)
                        high(1)
                        high(2)
                        fused(2)
                        high(3)
                        high(4)
                        nodes.root_on_scalar(act, 0)
                        nodes.relu_on_scalar(act, 0, h)
                        fused(3)
                        high(5)
                        act.wait_ge(deg_ready, 1)
                        act.activation(root[:, :], deg[:, :], ACT.Sqrt).then_inc(root_ready, 1)
                        high(6)

                    @block.vector
                    def _(dve):
                        link = Chain(dve, chain_p).link

                        def floor_div(to, scratch, a, by, mid_point):
                            link(dve.tensor_scalar(scratch[:, :], a[:, :], mid_point, 1.0 / by, ALU.subtract, ALU.mult))
                            link(dve.tensor_scalar(to[:, :], scratch[:, :], ROUND, ROUND, ALU.add, ALU.subtract))

                        def fma(to, a, by, plus):
                            link(dve.scalar_tensor_tensor(to[:, :], a[:, :], by, plus[:, :], ALU.mult, ALU.add))

                        dve.wait_ge(edges_in, 48)
                        dve.tensor_copy(dstf[:, :], ints[:, 0, :])
                        dve.tensor_copy(typef[:, :], ints[:, 1, :])
                        link(dve.tensor_copy(srcf[:, :], ints[:, 2, :]))
                        floor_div(blk, rank, dstf, BN, (BN - 1) / 2)
                        fma(bucket, blk, float(R), typef)
                        dve.wait_ge(consts, 1)

                        def one_hot(to, iota, k, a):
                            return dve.tensor_tensor(
                                to[:, :, :], iota[:, :].unsqueeze(1).to_broadcast([P, EJ, k]),
                                a[:, :].unsqueeze(2).to_broadcast([P, EJ, k]), ALU.is_equal)

                        link(one_hot(hot, iota_w, W, bucket))
                        link(dve.memset(before[:, 0, :], 0.0))
                        for i in range(1, EJ):
                            link(dve.tensor_tensor(before[:, i, :], before[:, i - 1, :], hot[:, i - 1, :], ALU.add))
                        dve.tensor_tensor(row_sum[:, :], before[:, EJ - 1, :], hot[:, EJ - 1, :], ALU.add)\
                            .then_inc(sums_ready, 1)
                        fma(loc, blk, -float(BN), dstf)
                        floor_div(prt, rank, loc, J, (J - 1) / 2)
                        fma(row4, prt, -float(J), loc)
                        fma(col, row4, float(P), prt)
                        fma(qidx, blk, float(J), row4)
                        for i, value in enumerate((srcf, col)):
                            link(dve.scalar_tensor_tensor(
                                pairs[:, :, i, :], value[:, :].unsqueeze(2).to_broadcast([P, EJ, W]), 1.0,
                                hot[:, :, :], ALU.add, ALU.mult))
                        dve.wait_ge(ranks_up, 2)
                        link(dve.tensor_tensor(before[:, :, :], before[:, :, :],
                                               p_rank[0:P, 0:W].unsqueeze(1).to_broadcast([P, EJ, W]), ALU.add))
                        link(dve.tensor_reduce(top[:, 0:1], p_count[:, 0:W], AX.X, ALU.max))
                        link(dve.tensor_scalar(top[:, 1:2], top[:, 0:1], (SLOTS - 1) / 2, 1.0 / SLOTS,
                                               ALU.add, ALU.mult))
                        link(dve.tensor_scalar(top[:, 0:1], top[:, 1:2], ROUND, ROUND, ALU.add, ALU.subtract))
                        link(dve.tensor_scalar(top[:, 1:2], top[:, 0:1], -1.0, 0.0, ALU.add, ALU.max))
                        dve.tensor_copy(rounds_sb[:, :], top[:, 1:2]).then_inc(rounds_ready, 1)
                        link(dve.tensor_scalar(top[:, 0:1], top[:, 1:2], float(SLOTS), None, ALU.mult))
                        link(dve.tensor_tensor(before[:, :, :], before[:, :, :], hot[:, :, :], ALU.mult))
                        link(dve.tensor_reduce(rank[:, :], before[:, :, :], AX.X, ALU.add))
                        link(dve.tensor_scalar(rank[:, :], rank[:, :], top[0:P, 0:1], None, ALU.subtract))
                        dve.wait_ge(consts, 2)
                        dve.wait_ge(rounds_ready, 1)
                        rounds = dve.value_load(rounds_sb[0:1, 0:1], min_val=0, max_val=MAXR - 1)

                        def choose():
                            dve.tensor_tensor(pick[:, :, :], iota_s[:, :].unsqueeze(1).to_broadcast([P, EJ, 128]),
                                              rank[:, :].unsqueeze(2).to_broadcast([P, EJ, 128]), ALU.is_equal)\
                                .then_inc(picked, 1)

                        def table(k, inner):
                            dve.wait_ge(slots_up, k + 1)
                            inner(dve.tensor_scalar(empty[:, :], p_slots[:, 0:W], 0.0, ABSENT, ALU.is_equal, ALU.mult))
                            inner(dve.scalar_tensor_tensor(slot_src, p_slots[:, 0:W], -1.0, empty[:, :],
                                                           ALU.add, ALU.add))
                            inner(dve.tensor_scalar(slot_col, p_slots[:, W:2 * W], -1.0, None, ALU.add))

                        choose()
                        with dve.If(rounds > 0):
                            with dve.Fori(0, rounds) as k:
                                inner = Chain(dve, slots_out, 4 * k).link
                                table(k, inner)
                                inner(dve.tensor_scalar(rank[:, :], rank[:, :], float(SLOTS), None, ALU.add))
                                choose()
                                dve.wait_ge(tables_free, k + 1)
                        one_hot(hot_p, iota_p, P, prt)
                        one_hot(hot_q, iota_q, NB * J, qidx).then_inc(hots_ready, 1)
                        dve.wait_ge(x_in, 32)
                        nodes.on_vector(dve, 0, h)
                        table(rounds, Chain(dve, slots_out, 4 * rounds).link)
                        dve.wait_ge(deg_up, 1)
                        dve.tensor_scalar(deg[:, :], p_deg[0:P, 0:NB * J], 1.0, None, ALU.add).then_inc(deg_ready, 1)
                        dve.wait_ge(cols_up, 1)
                        dve.tensor_copy(b1_col[:, :], p_cols[:, 0:STEPS])
                        dve.tensor_copy(bg_col[:, :], p_cols[:, 16:16 + KC]).then_inc(cols_copied, 1)
                        dve.wait_ge(bias_up, 1)
                        dve.tensor_copy(bias[:, :], p_count[:, :])
                        low_part(dve, 5)
                        dve.wait_ge(bias2_up, 1)
                        dve.tensor_copy(bias2[:, :], p_fuse[2][:, :]).then_inc(bias2_copied, 1)
                        dve.wait_ge(root_ready, 1)
                        link(dve.reciprocal(dinv[:, :], root[:, :]))
                        link(dve.tensor_tensor(y2[:, :], dinv[:, :], dinv[:, :], ALU.mult))
                        link(dve.tensor_tensor(y2[:, :], y2[:, :], deg[:, :], ALU.mult))
                        link(dve.tensor_scalar(y2[:, :], y2[:, :], -0.5, 1.5, ALU.mult, ALU.add))
                        link(dve.tensor_tensor(dinv[:, :], dinv[:, :], y2[:, :], ALU.mult))

                    @block.tensor
                    def _(pe):
                        def fuse(m):
                            pe.wait_ge(gt_copied, KC)
                            if m >= 2:
                                pe.wait_ge(fused_copied, m - 1)
                            for k in range(KC):
                                mm = pe.matmul(p_fuse[m % 2][:, :], gcn_t[:, k, m * 128:(m + 1) * 128], dense[:, k, :],
                                               start=(k == 0), stop=(k == KC - 1))
                            mm.then_inc(fused_up, 1)

                        pe.wait_ge(consts, 1)
                        pe.wait_ge(gcn_in, 16)
                        for k in range(KC):
                            if k >= 2:
                                pe.wait_ge(gt_copied, k - 1)
                            for m in range(KC):
                                mm = pe.transpose(p_fuse[k % 2][:, m * 128:(m + 1) * 128],
                                                  gcn[:, m, k * 128:(k + 1) * 128], ident[:, :])
                            mm.then_inc(gt_up, 1)
                        pe.wait_ge(sums_ready, 1)
                        pe.matmul(p_rank[0:P, 0:W], tri[:, :], row_sum[:, :], start=True, stop=True)\
                            .then_inc(ranks_up, 1)
                        pe.matmul(p_count[:, 0:W], ones[:, :], row_sum[:, :], start=True, stop=True)\
                            .then_inc(ranks_up, 1)
                        pe.wait_ge(dense_in, 16)
                        for m in range(KC - 1):
                            fuse(m)
                        pe.wait_ge(bias_in, 16 * 5)
                        pe.transpose(p_cols[:, 0:STEPS], b1_rows[:, :], ident[0:STEPS, 0:STEPS])
                        pe.transpose(p_cols[:, 16:16 + KC], bg_rows[:, :], ident[0:KC, 0:KC]).then_inc(cols_up, 1)
                        pe.wait_ge(rounds_ready, 1)
                        pe.matmul(p_count[:, :], ones[0:R + 1, :], bias_rows[:, :], start=True, stop=True)\
                            .then_inc(bias_up, 1)
                        rounds = pe.value_load(rounds_sb[0:1, 0:1], min_val=0, max_val=MAXR - 1)
                        with pe.Fori(0, rounds + 1) as k:
                            pe.wait_ge(picked, k + 1)
                            for i in range(EJ):
                                mm = pe.matmul(p_slots[:, 0:2 * W], pick[:, i, :],
                                               pairs[:, i, :, :].rearrange("p a w -> p (a w)"),
                                               start=(i == 0), stop=(i == EJ - 1))
                            mm.then_inc(slots_up, 1)
                        pe.wait_ge(hots_ready, 1)
                        for i in range(EJ):
                            mm = pe.matmul(p_deg[0:P, 0:NB * J], hot_p[:, i, :], hot_q[:, i, :],
                                           start=(i == 0), stop=(i == EJ - 1))
                        mm.then_inc(deg_up, 1)
                        fuse(KC - 1)
                        pe.wait_ge(cols_copied, 1)
                        for k in range(KC):
                            pe.matmul(p_fuse[2][:, :], bg_col[:, k:k + 1].to_broadcast([128, 128]),
                                      dense[:, k, :], start=(k == 0), stop=False)
                        pe.matmul(p_fuse[2][:, :], ones[0:1, :], dense_row[:, :], start=False, stop=True)\
                            .then_inc(bias2_up, 1)


        with layer0:
            res = sb("res0", [P, J, XW], F32, layer0)
            ht = sb("ht0", [128, KC, BN], F32, layer0)
            g_hi = [sb(f"g_hi{i}", [128, KC, BN], F32R, layer0) for i in range(R)]
            g_lo = [sb(f"g_lo{i}", [128, KC, BN], F32R, layer0) for i in range(R)]
            hid_hi = [sb(f"hid_hi{i}", [128, BN], F32R, layer0) for i in range(2)]
            hid_lo = [sb(f"hid_lo{i}", [128, BN], F32R, layer0) for i in range(2)]
            index = sb("index0", [128, 1], I32, layer0)
            rows = Rows("rows0", layer0, True)
            outs = Nodes("outs0", layer0, 1)
            more = Rounds("more0", layer0, x, Rows("more_rows0", layer0, True, rows))
            out_bank = [layer0.enter_context(nc.psum_tensor(f"out_bank{j}", [128, 512], F32)) for j in range(J)]
            hid_bank = [layer0.enter_context(nc.psum_tensor(f"hid_bank{i}", [128, 512], F32)) for i in range(2)]
            sum_bank = [layer0.enter_context(nc.psum_tensor(f"sum_bank{i}", [128, 512], F32)) for i in range(2)]

            fused_in, fused_high = sem("fused_in"), sem("fused_high")
            res_in, stored, cleared = sem("res_in"), sem("stored"), sem("cleared")
            indexed, gathers = sem("indexed"), sem("gathers")
            t_done, t_copied = sem("t_done"), sem("t_copied")
            self_high, self_ready, self_done = sem("self_high"), sem("self_ready"), sem("self_done")
            agg_done, agg_added = sem("agg_done"), sem("agg_added")
            g_high, g_ready = sem("g_high"), sem("g_ready")
            z_done, z_relued, z_high, hid_ready = (
                sem("z_done"), sem("z_relued"), sem("z_high"), sem("hid_ready"))
            c_done, evacuated, biased = sem("c_done"), sem("evacuated"), sem("biased")

            with nc.Block() as block:
                @block.sync
                def _(sp):
                    def load(to, b, signal):
                        for p0, p1 in PARTS:
                            sp.dma_start(to[p0:p1, :, 0:D], x_blocks[b, p0:p1, :, :]).then_inc(signal, 16)

                    def store(b):
                        sp.wait_ge(outs.norm_ready, b + 1)
                        for p0, p1 in PARTS:
                            sp.dma_start(mid_blocks[b, p0:p1, :, :], res[p0:p1, :, :]).then_inc(stored, 16)
                        sp.wait_ge(stored, 32 * (b + 1))

                    sp.wait_ge(cleared, 1)
                    load(res, 0, res_in)
                    with sp.Fori(0, NB - 1) as b:
                        sp.wait_ge(t_done, 2 * (b + 1))
                        load(h, b + 1, x_in)
                        store(b)
                        load(res, b + 1, res_in)
                    sp.wait_ge(t_done, 2 * NB)
                    sp.dma_start(h_wide[:, :, :].rearrange("p k n -> p (k n)"), fused_dram).then_inc(fused_in, 16)
                    store(NB - 1)

                @block.gpsimd
                def _(pool):
                    rounds = load_rounds(pool)
                    last_row = pool.to_reg(N - 1)
                    pool.memset(rows.x[:, :], 0.0).then_inc(indexed, 1)
                    pool.memset(res[:, :, D:XW], 0.0).then_inc(cleared, 1)

                    def gather(w):
                        pool.wait_ge(rows.ready, w + 1)
                        pool.wait_ge(more.done, KC * (rounds * w) + 1)
                        pool.wait_ge(indexed, w + 1)
                        pool.sem_inc(gathers, 1)
                        pool.tensor_copy(index[:, :], slot_src[:, bass.ds(w, 1)]).then_inc(indexed, 1)
                        pool.wait_ge(indexed, w + 2)
                        pool.sem_inc(gathers, 1)
                        pool.indirect_dma_start(rows.x[:, :], None, x, bass.IndirectOffsetOnAxis(index[:, :], 0),
                                                bounds_check=last_row, oob_is_err=False).then_inc(rows.gathered, 16)
                        more.on_gpsimd(pool, rounds, w, (g_ready, KC * (w + 1)), last_row)

                    def residual(b):
                        pool.wait_ge(res_in, 32 * (b + 1))
                        pool.tensor_tensor(res[:, :, 0:D], res[:, :, 0:D],
                                           bias[0:P, :].unsqueeze(1).to_broadcast([P, J, D]), ALU.add)
                        pool.tensor_copy(res[:, :, DINV], dinv[:, bass.ds(J * b, J)]).then_inc(biased, 1)

                    gather(0)
                    gather(1)
                    with pool.Fori(0, NB - 1) as b:
                        gather(R * b + 2)
                        residual(b)
                        gather(R * b + 3)
                        gather(R * b + 4)
                    gather(R * NB - 1)
                    residual(NB - 1)

                @block.scalar
                def _(act):
                    rounds = load_rounds(act)

                    def transposed(b, half, free):
                        for c in (2 * half, 2 * half + 1):
                            act.wait_ge(t_done, 2 * b + half + 1)
                            act.wait_ge(agg_added, KC * R * b)
                            act.activation(ht[:, c, :], sum_bank[c % 2][:, 0:BN], ACT.Copy).then_inc(t_copied, 1)
                        if free:
                            act.wait_ge(*free)
                        for c in (2 * half, 2 * half + 1):
                            act.wait_ge(t_copied, KC * b + 2 * half + 2)
                            act.activation(g_hi[1][:, c, :], ht[:, c, :], ACT.Copy).then_inc(self_high, 1)

                    def summed(w, r, half, free):
                        if free:
                            act.wait_ge(*free)
                        for c in (2 * half, 2 * half + 1):
                            act.wait_ge(agg_added, KC * w + c + 1)
                            act.activation(g_hi[r][:, c, :], sum_bank[c % 2][:, 0:BN], ACT.Copy).then_inc(g_high, 1)

                    def hidden(b, s):
                        n = STEPS * b + s
                        z = hid_bank[s % 2][:, 0:BN]
                        act.wait_ge(z_done, n + 1)
                        act.activation(z, z, ACT.Relu, bias=b1_col[:, s:s + 1]).then_inc(z_relued, 1)
                        act.wait_ge(z_relued, n + 1)
                        act.wait_ge(c_done, J * (n + 1))
                        act.activation(hid_hi[s % 2][:, :], z, ACT.Copy).then_inc(z_high, 1)

                    def body(b, more_blocks):
                        hidden(b, 1)
                        summed(R * b + 1, 1, 0, (self_done, b + 1))
                        hidden(b, 2)
                        summed(R * b + 1, 1, 1, None)
                        more.on_scalar(act, rounds, R * b + 1, sum_bank, g_hi[1])
                        rows.stats_on_scalar(act, R * b + 2)
                        hidden(b, 3)
                        rows.split_on_scalar(act, R * b + 2)
                        hidden(b, 4)
                        summed(R * b + 2, 2, 0, (z_done, STEPS * b + 1))
                        hidden(b, 5)
                        summed(R * b + 2, 2, 1, None)
                        more.on_scalar(act, rounds, R * b + 2, sum_bank, g_hi[2])
                        hidden(b, 6)
                        if more_blocks:
                            nodes.root_on_scalar(act, b + 1)
                        hidden(b, 7)
                        if more_blocks:
                            nodes.relu_on_scalar(act, b + 1, h)
                            rows.stats_on_scalar(act, R * (b + 1))
                        hidden(b, 8)
                        if more_blocks:
                            rows.split_on_scalar(act, R * (b + 1))
                            transposed(b + 1, 0, (z_done, STEPS * b + 2 * KC))
                        else:
                            act.wait_ge(fused_in, 16)
                            act.wait_ge(self_done, NB)
                            act.activation(ws_hi[:, :, :], h_wide[:, :, :], ACT.Copy).then_inc(fused_high, 1)
                        hidden(b, 9)
                        if more_blocks:
                            transposed(b + 1, 1, None)
                        hidden(b, 10)
                        if more_blocks:
                            summed(R * (b + 1), 0, 0, (z_done, STEPS * b + KC))
                        hidden(b, 11)
                        if more_blocks:
                            summed(R * (b + 1), 0, 1, None)
                            more.on_scalar(act, rounds, R * (b + 1), sum_bank, g_hi[0])
                        outs.root_on_scalar(act, b)
                        if more_blocks:
                            hidden(b + 1, 0)
                            rows.on_scalar(act, R * (b + 1) + 1)

                    transposed(0, 0, None)
                    transposed(0, 1, None)
                    rows.on_scalar(act, 0)
                    summed(0, 0, 0, None)
                    summed(0, 0, 1, None)
                    more.on_scalar(act, rounds, 0, sum_bank, g_hi[0])
                    hidden(0, 0)
                    rows.on_scalar(act, 1)
                    with act.Fori(0, NB - 1) as b:
                        body(b, True)
                    body(NB - 1, False)

                @block.vector
                def _(dve):
                    rounds = load_rounds(dve)

                    def own(b):
                        dve.wait_ge(x_in, 32 * (b + 1))
                        nodes.on_vector(dve, b, h)

                    def transposed(b, half):
                        for c in (2 * half, 2 * half + 1):
                            dve.wait_ge(self_high, KC * b + c + 1)
                            dve.tensor_tensor(g_lo[1][:, c, :], ht[:, c, :], g_hi[1][:, c, :].bitcast(F32), ALU.subtract)\
                                .then_inc(self_ready, 1)

                    def summed(w, r, half):
                        for c in (2 * half, 2 * half + 1):
                            bank = sum_bank[c % 2][:, 0:BN]
                            dve.wait_ge(agg_done, 2 * w + half + 1)
                            dve.tensor_tensor(bank, bank, ht[:, c, :], ALU.add).then_inc(agg_added, 1)
                        for c in (2 * half, 2 * half + 1):
                            dve.wait_ge(g_high, KC * w + c + 1)
                            dve.tensor_tensor(g_lo[r][:, c, :], sum_bank[c % 2][:, 0:BN],
                                              g_hi[r][:, c, :].bitcast(F32), ALU.subtract).then_inc(g_ready, 1)

                    def hidden(b, s):
                        n = STEPS * b + s
                        dve.wait_ge(z_high, n + 1)
                        dve.tensor_tensor(hid_lo[s % 2][:, :], hid_bank[s % 2][:, 0:BN],
                                          hid_hi[s % 2][:, :].bitcast(F32), ALU.subtract).then_inc(hid_ready, 1)

                    def evacuate(b):
                        dve.wait_ge(biased, b + 1)
                        for j in range(J):
                            dve.wait_ge(c_done, J * (STEPS * b + STEPS + 1) + j + 1)
                            dve.tensor_tensor(res[:, j, 0:D], res[:, j, 0:D], out_bank[j][0:P, :], ALU.add)\
                                .then_inc(evacuated, 1)

                    def stats(w):
                        dve.wait_ge(agg_done, 2 * w)
                        rows.stats_on_vector(dve, w, slot_col[:, bass.ds(w, 1)])

                    def body(b, more_blocks):
                        hidden(b, 1)
                        summed(R * b + 1, 1, 0)
                        hidden(b, 2)
                        summed(R * b + 1, 1, 1)
                        more.on_vector(dve, rounds, R * b + 1, sum_bank, g_hi[1], g_lo[1])
                        stats(R * b + 2)
                        hidden(b, 3)
                        rows.split_on_vector(dve, R * b + 2)
                        hidden(b, 4)
                        summed(R * b + 2, 2, 0)
                        hidden(b, 5)
                        summed(R * b + 2, 2, 1)
                        more.on_vector(dve, rounds, R * b + 2, sum_bank, g_hi[2], g_lo[2])
                        hidden(b, 6)
                        if more_blocks:
                            own(b + 1)
                        hidden(b, 7)
                        if more_blocks:
                            stats(R * (b + 1))
                        hidden(b, 8)
                        if more_blocks:
                            rows.split_on_vector(dve, R * (b + 1))
                            transposed(b + 1, 0)
                        else:
                            dve.wait_ge(fused_high, 1)
                            dve.tensor_tensor(ws_lo[:, :, :], h_wide[:, :, :], ws_hi[:, :, :].bitcast(F32), ALU.subtract)
                        hidden(b, 9)
                        if more_blocks:
                            transposed(b + 1, 1)
                        hidden(b, 10)
                        if more_blocks:
                            summed(R * (b + 1), 0, 0)
                        hidden(b, 11)
                        if more_blocks:
                            summed(R * (b + 1), 0, 1)
                            more.on_vector(dve, rounds, R * (b + 1), sum_bank, g_hi[0], g_lo[0])
                        evacuate(b)
                        dve.wait_ge(evacuated, J * (b + 1) + J)
                        outs.on_vector(dve, b, res)
                        if more_blocks:
                            hidden(b + 1, 0)
                            stats(R * (b + 1) + 1)
                            rows.split_on_vector(dve, R * (b + 1) + 1)

                    for ready in (rows.ready, more.done):
                        dve.sem_inc(ready, 1)
                    dve.sem_inc(evacuated, J)
                    dve.sem_inc(hid_ready, 2)
                    low_part(dve, len(weights) - 1)
                    transposed(0, 0)
                    transposed(0, 1)
                    stats(0)
                    rows.split_on_vector(dve, 0)
                    summed(0, 0, 0)
                    summed(0, 0, 1)
                    more.on_vector(dve, rounds, 0, sum_bank, g_hi[0], g_lo[0])
                    hidden(0, 0)
                    stats(1)
                    rows.split_on_vector(dve, 1)
                    with dve.Fori(0, NB - 1) as b:
                        body(b, True)
                    body(NB - 1, False)

                @block.tensor
                def _(pe):
                    rounds = load_rounds(pe)

                    def transpose(b, half):
                        pe.wait_ge(nodes.ready, J * (b + 1))
                        if half:
                            pe.wait_ge(t_copied, KC * b + 2)
                        else:
                            pe.wait_ge(g_ready, KC * R * b)
                        for c in (2 * half, 2 * half + 1):
                            for j in range(J):
                                mm = pe.transpose(sum_bank[c % 2][:, j * P:(j + 1) * P],
                                                  h[:, j, c * 128:(c + 1) * 128], ident[0:P, 0:P])
                        mm.then_inc(t_done, 1)

                    def aggregate(w, half, banks_free):
                        pe.wait_ge(rows.ready, w + 2)
                        pe.wait_ge(*banks_free)
                        for c in (2 * half, 2 * half + 1):
                            mm = pe.matmul(sum_bank[c % 2][:, 0:BN], rows.xr[:, c * 128:(c + 1) * 128],
                                           rows.select[:, :], start=True, stop=True)
                        mm.then_inc(agg_done, 1)

                    def first(b, s):
                        r, m = divmod(s, KC)
                        n = STEPS * b + s
                        if m == 0:
                            pe.wait_ge(g_ready, KC * (R * b + r + 1))
                        pe.wait_ge(hid_ready, n + 1)
                        for k in range(KC):
                            at = r * KC + k
                            mm = split_product(pe, hid_bank[s % 2][:, 0:BN],
                                               (w1_hi[:, at, m * 128:(m + 1) * 128], w1_lo[:, at, m * 128:(m + 1) * 128]),
                                               (g_hi[r][:, k, :], g_lo[r][:, k, :]), k == 0, k == KC - 1)
                        mm.then_inc(z_done, 1)

                    def own(b, nodes_of=range(J)):
                        pe.wait_ge(self_ready, KC * (b + 1))
                        for j in nodes_of:
                            pe.wait_ge(evacuated, J * b + j + 1)
                            for k in range(KC):
                                mm = split_product(pe, out_bank[j][0:P, :],
                                                   (g_hi[1][:, k, j * P:(j + 1) * P], g_lo[1][:, k, j * P:(j + 1) * P]),
                                                   (ws_hi[:, k, :], ws_lo[:, k, :]), k == 0, False)
                        if j == J - 1:
                            mm.then_inc(self_done, 1)

                    def second(b, s):
                        n = STEPS * b + s
                        pe.wait_ge(hid_ready, n + 3)
                        for j in range(J):
                            mm = split_product(pe, out_bank[j][0:P, :],
                                               (hid_hi[s % 2][:, j * P:(j + 1) * P], hid_lo[s % 2][:, j * P:(j + 1) * P]),
                                               (w2_hi[:, s, :], w2_lo[:, s, :]), False, s == STEPS - 1)
                            if s == STEPS - 1:
                                mm.then_inc(c_done, 1)
                        if s < STEPS - 1:
                            mm.then_inc(c_done, J)

                    def body(b, more_blocks):
                        w = R * b
                        first(b, 1)
                        second(b, 0)
                        aggregate(w + 1, 0, (g_ready, KC * (w + 1)))
                        first(b, 2)
                        second(b, 1)
                        aggregate(w + 1, 1, (g_ready, KC * (w + 1) + 2))
                        more.on_tensor(pe, rounds, w + 1, sum_bank)
                        first(b, 3)
                        second(b, 2)
                        first(b, 4)
                        second(b, 3)
                        aggregate(w + 2, 0, (g_ready, KC * (w + 2)))
                        first(b, 5)
                        second(b, 4)
                        aggregate(w + 2, 1, (g_ready, KC * (w + 2) + 2))
                        more.on_tensor(pe, rounds, w + 2, sum_bank)
                        for s in (6, 7, 8):
                            first(b, s)
                            second(b, s - 1)
                        if more_blocks:
                            transpose(b + 1, 0)
                        first(b, 9)
                        second(b, 8)
                        if more_blocks:
                            transpose(b + 1, 1)
                        first(b, 10)
                        second(b, 9)
                        if more_blocks:
                            aggregate(w + 3, 0, (t_copied, KC * (b + 2)))
                        first(b, 11)
                        second(b, 10)
                        if more_blocks:
                            aggregate(w + 3, 1, (g_ready, KC * (w + 3) + 2))
                            more.on_tensor(pe, rounds, w + 3, sum_bank)
                        second(b, 11)
                        if more_blocks:
                            first(b + 1, 0)
                            own(b + 1)

                    pe.sem_inc(c_done, 2 * J)
                    transpose(0, 0)
                    transpose(0, 1)
                    own(0, (0, 1))
                    aggregate(0, 0, (t_copied, KC))
                    own(0, (2,))
                    aggregate(0, 1, (g_ready, 2))
                    own(0, (3,))
                    more.on_tensor(pe, rounds, 0, sum_bank)
                    first(0, 0)
                    with pe.Fori(0, NB - 1) as b:
                        body(b, True)
                    body(NB - 1, False)

        layer1 = ExitStack()
        with layer1:
            RES, TURN, TILES = 4, 4, 2 * R
            h = sb("h1", [P, J, D], F32, layer1)
            res = [sb(f"res1_{i}", [P, J, XW], F32, layer1) for i in range(RES)]
            ht = sb("ht1", [128, KC, BN], F32, layer1)
            g_hi = [sb(f"u_hi{i}", [128, KC, BN], F32R, layer1) for i in range(2)]
            g_lo = [sb(f"u_lo{i}", [128, KC, BN], F32R, layer1) for i in range(2)]
            index = [sb(f"index1_{i}", [128, 1], I32, layer1) for i in range(TILES)]
            rows = [Rows(f"rows1_{i}", layer1, False) for i in range(TILES)]
            more = Rounds("more1", layer1, mid, Rows("more_rows1", layer1, False))
            out_bank = [layer1.enter_context(nc.psum_tensor(f"y_bank{j}", [128, 512], F32)) for j in range(J)]
            sum_bank = [layer1.enter_context(nc.psum_tensor(f"u_bank{c}", [128, 512], F32)) for c in range(KC)]

            bias_in, cleared, cleared_first = sem("bias_in1"), sem("cleared1"), sem("cleared_first")
            res_in = [sem(f"mid_in{i}") for i in range(RES)]
            stored = [sem(f"out_stored{i}") for i in range(RES)]
            indexed, gathers = sem("indexed1"), sem("gathers1")
            rows_used = sem("rows_used1")
            h_ready, t_done, t_copied = sem("h_ready1"), sem("t_done1"), sem("t_copied1")
            agg_added, g_high, g_ready = sem("agg_added1"), sem("g_high1"), sem("g_ready1")
            out_done, evacuated, biased = sem("out_done1"), sem("evacuated1"), sem("biased1")

            def tile_of(r, turn, place):
                return rows[R * (place % 2) + r], TURN // 2 * turn + place // 2

            def turns(engine, body):
                with engine.Fori(0, NB // TURN - 1) as t:
                    for i in range(TURN):
                        body(TURN * t + i, t, i, NB)
                for i in range(TURN):
                    body(NB - TURN + i, NB // TURN - 1, i, TURN - i)

            with nc.Block() as block:
                @block.sync
                def _(sp):
                    def load(b, slot):
                        for p0, p1 in PARTS:
                            sp.dma_start(res[slot][p0:p1, :, :], mid_blocks[b, p0:p1, :, :]).then_inc(res_in[slot], 16)

                    def body(b, turn, i, left):
                        if left == 1:
                            for j in range(J):
                                sp.wait_ge(evacuated, J * b + J + j + 1)
                                for p0, p1 in PARTS:
                                    sp.dma_start(out_blocks[b, p0:p1, j, :], res[i][p0:p1, j, 0:D])\
                                        .then_inc(stored[i], 16)
                            sp.wait_ge(stored[i], 32 * (turn + J))
                            return
                        sp.wait_ge(evacuated, J * (b + 1) + J)
                        for p0, p1 in PARTS:
                            sp.dma_start(out_blocks[b, p0:p1, :, :], res[i][p0:p1, :, 0:D]).then_inc(stored[i], 16)
                        sp.wait_ge(stored[i], 32 * (turn + 1))
                        if left > RES:
                            load(b + RES, i)

                    load(0, 0)
                    sp.dma_start(bias[:, :], bias2_dram).then_inc(bias_in, 16)
                    sp.wait_ge(rows[R - 1].gathered, 16)
                    for i in range(1, RES):
                        load(i, i)
                    turns(sp, body)

                @block.gpsimd
                def _(pool):
                    rounds = load_rounds(pool)
                    last_row = pool.to_reg(N - 1)

                    def gather(b, place):
                        for r in range(R):
                            w, tile = R * b + r, R * (place % 2) + r
                            pool.wait_ge(rows_used, w + 1)
                            pool.tensor_copy(index[tile][:, :], slot_src[:, bass.ds(w, 1)]).then_inc(indexed, 1)
                            pool.wait_ge(indexed, w + 1)
                            pool.sem_inc(gathers, 1)
                            pool.indirect_dma_start(rows[tile].x[:, :], None, mid,
                                                    bass.IndirectOffsetOnAxis(index[tile][:, :], 0),
                                                    bounds_check=last_row, oob_is_err=False)\
                                .then_inc(rows[tile].gathered, 16)

                    def add_bias(b, place):
                        pool.wait_ge(h_ready, J * (b + 1))
                        to = res[place % RES]
                        pool.tensor_tensor(to[:, :, 0:D], to[:, :, 0:D],
                                           bias[0:P, :].unsqueeze(1).to_broadcast([P, J, D]), ALU.add)\
                            .then_inc(biased, 1)

                    def body(b, turn, i, left):
                        if left > 2:
                            gather(b + 2, i + 2)
                        if left > 1:
                            add_bias(b + 1, i + 1)
                            for r in range(R):
                                more.on_gpsimd(pool, rounds, R * (b + 1) + r, (g_ready, KC * (b + 2)), last_row)

                    pool.memset(rows[0].x[:, :], 0.0).then_inc(cleared_first, 1)
                    pool.wait_ge(cleared_first, 1)
                    pool.wait_ge(cleared, R - 1)
                    gather(0, 0)
                    pool.wait_ge(cleared, TILES)
                    gather(1, 1)
                    pool.wait_ge(bias_in, 16)
                    add_bias(0, 0)
                    for r in range(R):
                        more.on_gpsimd(pool, rounds, r, (g_ready, KC), last_row)
                    turns(pool, body)

                @block.scalar
                def _(act):
                    rounds = load_rounds(act)

                    def own(b, turn, place):
                        slot = place % RES
                        act.wait_ge(res_in[slot], 32 * (turn + place // RES + 1))
                        for j in range(J):
                            act.activation(h[:, j, :], res[slot][:, j, 0:D], ACT.Relu,
                                           bias=res[slot][:, j, SHIFT:SHIFT + 1],
                                           scale=res[slot][:, j, SCALE:SCALE + 1]).then_inc(h_ready, 1)

                    def split(turn, place):
                        for r in range(R):
                            tile, n = tile_of(r, turn, place)
                            tile.on_scalar(act, n)

                    def transposed(b):
                        for c in range(KC):
                            act.wait_ge(t_done, KC * b + c + 1)
                            act.activation(ht[:, c, :], sum_bank[c][:, 0:BN], ACT.Copy).then_inc(t_copied, 1)

                    def summed(b, place):
                        for c in range(KC):
                            act.wait_ge(agg_added, KC * b + c + 1)
                            act.activation(g_hi[place % 2][:, c, :], sum_bank[c][:, 0:BN], ACT.Copy).then_inc(g_high, 1)
                        for r in range(R):
                            more.on_scalar(act, rounds, R * b + r, sum_bank, g_hi[place % 2])

                    def body(b, turn, i, left):
                        if left > 1:
                            act.wait_ge(out_done, J * b + 1)
                            summed(b + 1, i + 1)
                        if left > 2:
                            split(turn, i + 2)
                            transposed(b + 2)
                        if left > 3:
                            own(b + 3, turn, i + 3)

                    own(0, 0, 0)
                    split(0, 0)
                    act.wait_ge(t_done, KC)
                    own(1, 0, 1)
                    summed(0, 0)
                    transposed(1)
                    split(0, 1)
                    own(2, 0, 2)
                    turns(act, body)

                @block.vector
                def _(dve):
                    rounds = load_rounds(dve)

                    def split(b, turn, place):
                        for r in range(R):
                            tile, n = tile_of(r, turn, place)
                            dve.wait_ge(rows_used, R * b + r + 1)
                            tile.on_vector(dve, n, slot_col[:, bass.ds(R * b + r, 1)])

                    def summed(b, place):
                        hi, lo = g_hi[place % 2], g_lo[place % 2]
                        dve.wait_ge(rows_used, R * (b + 1) + TILES)
                        for c in range(KC):
                            bank = sum_bank[c][:, 0:BN]
                            dve.tensor_tensor(bank, bank, ht[:, c, :], ALU.add).then_inc(agg_added, 1)
                        for c in range(KC):
                            dve.wait_ge(g_high, KC * b + c + 1)
                            dve.tensor_tensor(lo[:, c, :], sum_bank[c][:, 0:BN], hi[:, c, :].bitcast(F32),
                                              ALU.subtract).then_inc(g_ready, 1)
                        for r in range(R):
                            more.on_vector(dve, rounds, R * b + r, sum_bank, hi, lo)

                    def evacuate(b, i):
                        dve.wait_ge(biased, b + 1)
                        for j in range(J):
                            dve.wait_ge(out_done, J * b + j + 2)
                            dve.scalar_tensor_tensor(res[i][:, j, 0:D], out_bank[j][0:P, :], res[i][:, j, DINV:DINV + 1],
                                                     res[i][:, j, 0:D], ALU.mult, ALU.add).then_inc(evacuated, 1)

                    def body(b, turn, i, left):
                        if left > 1:
                            summed(b + 1, i + 1)
                        if left > 2:
                            split(b + 2, turn, i + 2)
                        evacuate(b, i)

                    for tile in (*rows[1:], more.rows):
                        dve.memset(tile.x[:, :], 0.0).then_inc(cleared, 1)
                    dve.sem_inc(evacuated, J)
                    dve.sem_inc(more.done, 1)
                    for c in range(KC):
                        dve.wait_ge(t_done, c + 1)
                        dve.tensor_copy(ht[:, c, :], sum_bank[c][:, 0:BN]).then_inc(t_copied, 1)
                    split(0, 0, 0)
                    summed(0, 0)
                    split(1, 0, 1)
                    turns(dve, body)

                @block.tensor
                def _(pe):
                    rounds = load_rounds(pe)

                    def transpose(b, first=False):
                        pe.wait_ge(h_ready, J * (b + 1))
                        for c in range(KC):
                            if not first:
                                pe.wait_ge(g_ready, KC * (b - 1) + c + 1)
                            for j in range(J):
                                mm = pe.transpose(sum_bank[c][:, j * P:(j + 1) * P],
                                                  h[:, j, c * 128:(c + 1) * 128], ident[0:P, 0:P])
                            mm.then_inc(t_done, 1)

                    def aggregate(b, turn, place):
                        for r in range(R):
                            tile, n = tile_of(r, turn, place)
                            pe.wait_ge(tile.ready, n + 1)
                            for c in range(KC):
                                if r == 0:
                                    pe.wait_ge(t_copied, KC * b + c + 1)
                                mm = pe.matmul(sum_bank[c][:, 0:BN], tile.xr[:, c * 128:(c + 1) * 128],
                                               tile.select[:, :], start=(r == 0), stop=(r == R - 1))
                            mm.then_inc(rows_used, 1)
                        for r in range(R):
                            more.on_tensor(pe, rounds, R * b + r, sum_bank)

                    def multiply(b, i, j):
                        pe.wait_ge(evacuated, J * b + j + 1)
                        for k in range(KC):
                            mm = split_product(pe, out_bank[j][0:P, :],
                                               (g_hi[i % 2][:, k, j * P:(j + 1) * P],
                                                g_lo[i % 2][:, k, j * P:(j + 1) * P]),
                                               (ws_hi[:, k, :], ws_lo[:, k, :]), k == 0, k == KC - 1)
                        mm.then_inc(out_done, 1)

                    def body(b, turn, i, left):
                        if left > 1:
                            aggregate(b + 1, turn, i + 1)
                        pe.wait_ge(g_ready, KC * (b + 1))
                        for j in range(J - 1):
                            multiply(b, i, j)
                        if left > 2:
                            transpose(b + 2)
                        multiply(b, i, J - 1)

                    pe.sem_inc(rows_used, TILES)
                    pe.sem_inc(out_done, 1)
                    transpose(0, True)
                    aggregate(0, 0, 0)
                    transpose(1)
                    turns(pe, body)


_INS = ['x', 'src', 'dst', 'edge_type_3', 'L0_gnn_W_self', 'L0_gnn_b_self', 'L0_gnn_W1', 'L0_gnn_b1',
        'L0_gnn_W2', 'L0_gnn_b2', 'L1_gnn_W_gcn', 'L1_gnn_b_gcn', 'L1_gnn_W_dense', 'L1_gnn_b_dense']


def kernel(**inputs):
    import numpy as np
    import concourse.bacc as bacc
    from concourse.bass_utils import run_bass_kernel_spmd

    nc = bacc.Bacc("TRN2", target_bir_lowering=False, num_devices=1)
    arrays = {f"in_{name}": np.ascontiguousarray(inputs[name]) for name in _INS}
    args = [nc.dram_tensor(name, a.shape, mybir.dt.from_np(a.dtype), kind="ExternalInput").ap()
            for name, a in arrays.items()]
    out = nc.dram_tensor("out", arrays["in_x"].shape, mybir.dt.float32, kind="ExternalOutput").ap()
    build_program(nc, *args, out)
    return run_bass_kernel_spmd(nc, [arrays], core_ids=[0]).results[0]["out"]
```
